# Optimizing a Trainium2 kernel written in Bass

```python
import numpy as np
import jax
import jax.numpy as jnp

def _softmax(x, axis=-1):
    return jax.nn.softmax(x, axis=axis)

def _gelu(x):
    return jax.nn.gelu(x, approximate=True)

def _silu(x):
    return jax.nn.silu(x)

def _sigmoid(x):
    return jax.nn.sigmoid(x)

def _layernorm(x, axis=-1, eps=1e-05):
    m = jnp.mean(x, axis=axis, keepdims=True)
    v = jnp.var(x, axis=axis, keepdims=True)
    return (x - m) / jnp.sqrt(v + eps)

def _scatter_add(tgt, idx, src, axis=0):
    return tgt.at[idx].add(src)

def _segment_sum(src, seg, n):
    return jax.ops.segment_sum(src, seg, n)
kernel_name = 'mk_xattn_seq_d2_seqx_r4_7d4b79'

def setup_inputs(seed: int=0):
    np.random.seed(seed)
    _w = jnp.asarray

    def _rec_inputs():
        import jax
        import jax.numpy as jnp
        _rk = jax.random.key(seed)
        x = 0.0003765 + 1 * jax.random.normal(jax.random.fold_in(_rk, 1), (8, 256, 256), jnp.float32)
        _lenS = 256 - jax.random.randint(jax.random.fold_in(_rk, 7), (8,), 0, max(1, 256 // 4) + 1, jnp.int32)
        _lenS2 = 256 - jax.random.randint(jax.random.fold_in(_rk, 8), (8,), 0, max(1, 256 // 4) + 1, jnp.int32)
        _ctx_1024P = jax.random.normal(jax.random.fold_in(_rk, 11), (8, 16, 256), jnp.float32)
        _ctx_1024c = jax.random.dirichlet(jax.random.fold_in(_rk, 511), 0.3 * jnp.ones((16,), jnp.float32), (8, 256))
        _ctx_1024t = jnp.einsum('bsk,bkd->bsd', _ctx_1024c, _ctx_1024P)
        _ctx_1024t = _ctx_1024t * jax.lax.rsqrt(jnp.mean(jnp.square(_ctx_1024t)) + 1e-12) * 0.953939
        ctx_1024 = -0.000292821 + 1.00034 * (_ctx_1024t + 0.3 * jax.random.normal(jax.random.fold_in(_rk, 611), (8, 256, 256), jnp.float32))
        _validS = jnp.arange(256)[None, :] < _lenS[:, None]
        _validS2 = jnp.arange(256)[None, :] < _lenS2[:, None]
        _causal = jnp.tril(jnp.ones((256, 256), dtype=bool))
        mask_BxS_bf1 = jnp.ones((8, 256), dtype=bool)
        return (x, ctx_1024, mask_BxS_bf1)
    x, ctx_1024, mask_BxS_bf1 = _rec_inputs()

    def _L0_xattn_setup():
        import jax, jax.numpy as jnp
        import numpy as np
        EMB = 256
        HEADS = 16
        EPS = 1e-06
        key = jax.random.key(seed)
        ks = jax.random.split(key, 12)
        B, S, D = (2, 512, EMB)
        scale = 1.0 / np.sqrt(D)
        inp = {'v': jax.random.normal(ks[0], (B, S, D), jnp.float32), 'k': jax.random.normal(ks[1], (B, S, D), jnp.float32), 'q': jax.random.normal(ks[2], (B, S, D), jnp.float32), 'Wv': jax.random.normal(ks[3], (D, D), jnp.float32) * scale, 'bv': jnp.zeros((D,), jnp.float32), 'Wk': jax.random.normal(ks[4], (D, D), jnp.float32) * scale, 'bk': jnp.zeros((D,), jnp.float32), 'Wq': jax.random.normal(ks[5], (D, D), jnp.float32) * scale, 'bq': jnp.zeros((D,), jnp.float32), 'Wo': jax.random.normal(ks[6], (D, D), jnp.float32) * scale, 'bo': jnp.zeros((D,), jnp.float32), 'gamma': jnp.ones((D,), jnp.float32), 'beta': jnp.zeros((D,), jnp.float32)}
        return inp
    _L0_xattn_all = _L0_xattn_setup()
    _L0_xattn_in = {k: v for k, v in _L0_xattn_all.items() if k in ('Wv', 'bv', 'Wk', 'bk', 'Wq', 'bq', 'Wo', 'bo', 'gamma', 'beta')}
    del _L0_xattn_all

    def _L1_xattn_setup():
        import jax, jax.numpy as jnp
        import numpy as np
        D = 256
        H = 16
        DH = D // H
        FF = 4 * D
        EPS = 1e-05

        def masked_softmax(scores, mask=None):
            e = jnp.exp(jnp.clip(scores, -50.0, 50.0))
            if mask is not None:
                e = jnp.where(mask, e, 0.0)
            d = jnp.sum(e, axis=-1, keepdims=True)
            d = jnp.where(d <= 0.0, 1.0, d)
            return e / d

        def mha(q_in, k_in, v_in, wq, wk, wv, wo, mask=None):
            B = q_in.shape[0]
            q = (q_in @ wq).reshape(B, -1, H, DH).transpose(0, 2, 1, 3)
            k = (k_in @ wk).reshape(B, -1, H, DH).transpose(0, 2, 1, 3)
            v = (v_in @ wv).reshape(B, -1, H, DH).transpose(0, 2, 1, 3)
            scores = jnp.einsum('bhqd,bhkd->bhqk', q, k) / DH ** 0.5
            if mask is not None:
                mask = mask[:, None, :, None]
            attn = masked_softmax(scores, mask)
            out = jnp.einsum('bhqk,bhkd->bhqd', attn, v)
            out = out.transpose(0, 2, 1, 3).reshape(B, -1, D)
            return out @ wo

        def layer_norm(x, g, b):
            mu = jnp.mean(x, axis=-1, keepdims=True)
            var = jnp.mean(jnp.square(x - mu), axis=-1, keepdims=True)
            return (x - mu) / jnp.sqrt(var + EPS) * g + b
        key = jax.random.key(seed)
        ks = jax.random.split(key, 16)
        s = 0.02
        inp = {'main_seq': jax.random.normal(ks[0], (2, 512, D), jnp.float32), 'condition_seq': jax.random.normal(ks[1], (2, 128, D), jnp.float32), 'mask': jnp.ones((2, 512), dtype=bool), 'sa_wq': jax.random.normal(ks[2], (D, D), jnp.float32) * s, 'sa_wk': jax.random.normal(ks[3], (D, D), jnp.float32) * s, 'sa_wv': jax.random.normal(ks[4], (D, D), jnp.float32) * s, 'sa_wo': jax.random.normal(ks[5], (D, D), jnp.float32) * s, 'ca_wq': jax.random.normal(ks[6], (D, D), jnp.float32) * s, 'ca_wk': jax.random.normal(ks[7], (D, D), jnp.float32) * s, 'ca_wv': jax.random.normal(ks[8], (D, D), jnp.float32) * s, 'ca_wo': jax.random.normal(ks[9], (D, D), jnp.float32) * s, 'w1': jax.random.normal(ks[10], (D, FF), jnp.float32) * s, 'b1': jnp.zeros((FF,), jnp.float32), 'w2': jax.random.normal(ks[11], (FF, D), jnp.float32) * s, 'b2': jnp.zeros((D,), jnp.float32), 'g1': jnp.ones((D,), jnp.float32), 'be1': jnp.zeros((D,), jnp.float32), 'g2': jnp.ones((D,), jnp.float32), 'be2': jnp.zeros((D,), jnp.float32), 'g3': jnp.ones((D,), jnp.float32), 'be3': jnp.zeros((D,), jnp.float32)}
        return inp
    _L1_xattn_all = _L1_xattn_setup()
    _L1_xattn_in = {k: v for k, v in _L1_xattn_all.items() if k in ('sa_wq', 'sa_wk', 'sa_wv', 'sa_wo', 'ca_wq', 'ca_wk', 'ca_wv', 'ca_wo', 'w1', 'b1', 'w2', 'b2', 'g1', 'be1', 'g2', 'be2', 'g3', 'be3')}
    del _L1_xattn_all
    return {'x': x, 'ctx_1024': ctx_1024, 'mask_BxS_bf1': mask_BxS_bf1, 'L0_xattn_Wv': _L0_xattn_in['Wv'], 'L0_xattn_bv': _L0_xattn_in['bv'], 'L0_xattn_Wk': _L0_xattn_in['Wk'], 'L0_xattn_bk': _L0_xattn_in['bk'], 'L0_xattn_Wq': _L0_xattn_in['Wq'], 'L0_xattn_bq': _L0_xattn_in['bq'], 'L0_xattn_Wo': _L0_xattn_in['Wo'], 'L0_xattn_bo': _L0_xattn_in['bo'], 'L0_xattn_gamma': _L0_xattn_in['gamma'], 'L0_xattn_beta': _L0_xattn_in['beta'], 'L1_xattn_sa_wq': _L1_xattn_in['sa_wq'], 'L1_xattn_sa_wk': _L1_xattn_in['sa_wk'], 'L1_xattn_sa_wv': _L1_xattn_in['sa_wv'], 'L1_xattn_sa_wo': _L1_xattn_in['sa_wo'], 'L1_xattn_ca_wq': _L1_xattn_in['ca_wq'], 'L1_xattn_ca_wk': _L1_xattn_in['ca_wk'], 'L1_xattn_ca_wv': _L1_xattn_in['ca_wv'], 'L1_xattn_ca_wo': _L1_xattn_in['ca_wo'], 'L1_xattn_w1': _L1_xattn_in['w1'], 'L1_xattn_b1': _L1_xattn_in['b1'], 'L1_xattn_w2': _L1_xattn_in['w2'], 'L1_xattn_b2': _L1_xattn_in['b2'], 'L1_xattn_g1': _L1_xattn_in['g1'], 'L1_xattn_be1': _L1_xattn_in['be1'], 'L1_xattn_g2': _L1_xattn_in['g2'], 'L1_xattn_be2': _L1_xattn_in['be2'], 'L1_xattn_g3': _L1_xattn_in['g3'], 'L1_xattn_be3': _L1_xattn_in['be3']}

def reference(x, ctx_1024, mask_BxS_bf1, L0_xattn_Wv, L0_xattn_bv, L0_xattn_Wk, L0_xattn_bk, L0_xattn_Wq, L0_xattn_bq, L0_xattn_Wo, L0_xattn_bo, L0_xattn_gamma, L0_xattn_beta, L1_xattn_sa_wq, L1_xattn_sa_wk, L1_xattn_sa_wv, L1_xattn_sa_wo, L1_xattn_ca_wq, L1_xattn_ca_wk, L1_xattn_ca_wv, L1_xattn_ca_wo, L1_xattn_w1, L1_xattn_b1, L1_xattn_w2, L1_xattn_b2, L1_xattn_g1, L1_xattn_be1, L1_xattn_g2, L1_xattn_be2, L1_xattn_g3, L1_xattn_be3):
    import jax
    import jax.numpy as jnp

    def _L0_xattn_ref(v, k, q, Wv, bv, Wk, bk, Wq, bq, Wo, bo, gamma, beta):
        import jax, jax.numpy as jnp
        import numpy as np
        EMB = 256
        HEADS = 16
        EPS = 1e-06
        B, S, D = q.shape
        H = HEADS
        d = D // H

        def split_heads(x):
            return x.reshape(B, S, H, d).transpose(0, 2, 1, 3)
        V = split_heads(v @ Wv + bv)
        K = split_heads(k @ Wk + bk)
        Q = split_heads(q @ Wq + bq)
        scores = jnp.einsum('bhqd,bhkd->bhqk', Q, K) / jnp.sqrt(jnp.float32(d))
        attn = jax.nn.softmax(scores, axis=-1)
        ctx = jnp.einsum('bhqk,bhkd->bhqd', attn, V)
        ctx = ctx.transpose(0, 2, 1, 3).reshape(B, S, D)
        out = ctx @ Wo + bo + q
        mu = jnp.mean(out, axis=-1, keepdims=True)
        var = jnp.var(out, axis=-1, keepdims=True)
        return gamma * (out - mu) * jax.lax.rsqrt(var + EPS) + beta

    def _L1_xattn_ref(main_seq, condition_seq, mask, sa_wq, sa_wk, sa_wv, sa_wo, ca_wq, ca_wk, ca_wv, ca_wo, w1, b1, w2, b2, g1, be1, g2, be2, g3, be3):
        import jax, jax.numpy as jnp
        import numpy as np
        D = 256
        H = 16
        DH = D // H
        FF = 4 * D
        EPS = 1e-05

        def masked_softmax(scores, mask=None):
            e = jnp.exp(jnp.clip(scores, -50.0, 50.0))
            if mask is not None:
                e = jnp.where(mask, e, 0.0)
            d = jnp.sum(e, axis=-1, keepdims=True)
            d = jnp.where(d <= 0.0, 1.0, d)
            return e / d

        def mha(q_in, k_in, v_in, wq, wk, wv, wo, mask=None):
            B = q_in.shape[0]
            q = (q_in @ wq).reshape(B, -1, H, DH).transpose(0, 2, 1, 3)
            k = (k_in @ wk).reshape(B, -1, H, DH).transpose(0, 2, 1, 3)
            v = (v_in @ wv).reshape(B, -1, H, DH).transpose(0, 2, 1, 3)
            scores = jnp.einsum('bhqd,bhkd->bhqk', q, k) / DH ** 0.5
            if mask is not None:
                mask = mask[:, None, :, None]
            attn = masked_softmax(scores, mask)
            out = jnp.einsum('bhqk,bhkd->bhqd', attn, v)
            out = out.transpose(0, 2, 1, 3).reshape(B, -1, D)
            return out @ wo

        def layer_norm(x, g, b):
            mu = jnp.mean(x, axis=-1, keepdims=True)
            var = jnp.mean(jnp.square(x - mu), axis=-1, keepdims=True)
            return (x - mu) / jnp.sqrt(var + EPS) * g + b
        a = mha(main_seq, main_seq, main_seq, sa_wq, sa_wk, sa_wv, sa_wo, mask)
        x = layer_norm(main_seq + a, g1, be1)
        a = mha(x, condition_seq, condition_seq, ca_wq, ca_wk, ca_wv, ca_wo, None)
        x = layer_norm(x + a, g2, be2)
        ff = jax.nn.gelu(x @ w1 + b1, approximate=False) @ w2 + b2
        x = layer_norm(x + ff, g3, be3)
        return x
    x = _L0_xattn_ref(ctx_1024, ctx_1024, x, L0_xattn_Wv, L0_xattn_bv, L0_xattn_Wk, L0_xattn_bk, L0_xattn_Wq, L0_xattn_bq, L0_xattn_Wo, L0_xattn_bo, L0_xattn_gamma, L0_xattn_beta)
    x = _L1_xattn_ref(x, ctx_1024, mask_BxS_bf1, L1_xattn_sa_wq, L1_xattn_sa_wk, L1_xattn_sa_wv, L1_xattn_sa_wo, L1_xattn_ca_wq, L1_xattn_ca_wk, L1_xattn_ca_wv, L1_xattn_ca_wo, L1_xattn_w1, L1_xattn_b1, L1_xattn_w2, L1_xattn_b2, L1_xattn_g1, L1_xattn_be1, L1_xattn_g2, L1_xattn_be2, L1_xattn_g3, L1_xattn_be3)
    return x

_drawn_inputs = setup_inputs


def setup_inputs(seed=0):
    import zlib

    import numpy as np

    out = dict(_drawn_inputs(seed))
    spreads = {'L0_xattn_bv': (0.0, 0.1),
     'L0_xattn_bk': (0.0, 0.8),
     'L0_xattn_bq': (0.0, 0.394),
     'L0_xattn_bo': (0.0, 0.1),
     'L0_xattn_gamma': (1.0, 0.2),
     'L0_xattn_beta': (0.0, 0.1),
     'L1_xattn_b1': (0.0, 0.1),
     'L1_xattn_b2': (0.0, 0.1),
     'L1_xattn_g1': (1.0, 0.2),
     'L1_xattn_be1': (0.0, 0.1),
     'L1_xattn_g2': (1.0, 0.2),
     'L1_xattn_be2': (0.0, 0.1),
     'L1_xattn_g3': (1.0, 0.2),
     'L1_xattn_be3': (0.0, 0.1)}
    factors = {'L1_xattn_sa_wq': 8.0, 'L1_xattn_sa_wk': 8.0, 'L1_xattn_ca_wq': 8.0, 'L1_xattn_ca_wk': 8.0}
    for name, (base, spread) in spreads.items():
        noise = np.random.default_rng([zlib.crc32(name.encode()), seed]).standard_normal(out[name].shape)
        drawn = base * np.exp(spread * noise) if base else spread * noise
        out[name] = jnp.asarray(drawn.astype(out[name].dtype))
    for name, factor in factors.items():
        out[name] = (out[name] * factor).astype(out[name].dtype)
    return out
```

```python
from contextlib import ExitStack

import numpy as np

import concourse.bass as bass
from concourse import mybir

F32 = mybir.dt.float32
BF16 = mybir.dt.bfloat16
U8 = mybir.dt.uint8
ACT = mybir.ActivationFunctionType
ALU = mybir.AluOpType
AX_X = mybir.AxisListType.X

P = 128
B, S, D = 8, 256, 256
H = 16
DH = D // H
FF = 4 * D
T = S // P
KT = D // P
SCALE = float(DH) ** -0.5
Q_PARTS = (0, 0, 0, 1, 1, 2)
K_PARTS = (0, 1, 2, 0, 1, 0)
ROWS = DH * len(Q_PARTS)
MAX_ROW = ROWS
NPART = 3
QUADS = H // 4
CLIP_LO, CLIP_HI = float(np.exp(np.float32(-50.0))), float(np.exp(np.float32(50.0)))


def over_batch(engine, step):
    for b in range(2):
        step(b, b % 2, b == 0, False)
    with engine.Fori(0, (B - 4) // 2) as pair:
        for j in range(2):
            step(pair * 2 + (2 + j), j, False, False)
    for b in range(B - 2, B):
        step(b, b % 2, False, b == B - 1)


def after(engine, sem, value):
    if not isinstance(value, int) or value > 0:
        engine.wait_ge(sem, value)


def reached(engine, seen, sem, value):
    if not isinstance(value, int) or value > 0:
        engine.wait_ge(sem, value)
        engine.sem_inc(seen, 1)


class Chain:

    def __init__(self, engine, sem, per_b):
        self.engine, self.sem, self.per_b = engine, sem, per_b

    def start(self, b, k=0):
        self.b, self.k = b, k

    def link(self, ins):
        self.k += 1
        ins.then_inc(self.sem, 1)
        self.engine.wait_ge(self.sem, self.b * self.per_b + self.k)

    def end(self):
        assert self.k == self.per_b, (self.k, self.per_b)


def setup(nc, m, mask, ident_f, ident_b):
    with ExitStack() as ctx:
        filled = ctx.enter_context(nc.semaphore("setup_filled"))
        mask_in = ctx.enter_context(nc.semaphore("setup_mask_in"))
        block = ctx.enter_context(nc.Block())

        @block.sync
        def _(sp):
            sp.dma_start(m.mask_u8[:], mask.rearrange("b (t p) -> p b t", p=P)).then_inc(mask_in, 16)
            sp.wait_ge(mask_in, 16)

        @block.gpsimd
        def _(pool):
            nc.gpsimd.memset(ident_f[:], 0.0)
            nc.gpsimd.memset(ident_b[:], 0.0).then_inc(filled, 1)
            pool.wait_ge(filled, 1)
            for ident in (ident_f, ident_b):
                nc.gpsimd.affine_select(out=ident[:], in_=ident[:], compare_op=ALU.not_equal, fill=1.0,
                                        base=0, pattern=[[-1, P]], channel_multiplier=1)

        @block.vector
        def _(dve):
            for par in range(2):
                nc.vector.memset(m.vaug[par][:], 1.0)
                nc.vector.memset(m.kp[par][MAX_ROW:MAX_ROW + 32], 1.0)
            nc.vector.memset(m.neg_half[:], -0.5)
            for eps, tile in m.eps.items():
                nc.vector.memset(tile[:], eps)
            nc.vector.memset(m.mparts[:], 0.0)
            dve.wait_ge(mask_in, 16)
            nc.vector.tensor_copy(m.maskf[:], m.mask_u8[:])


def attention_phase(nc, m, name, q_src, kv_src, x_out, w, softmax_max, use_mask, eps, loads):
    has_bias = softmax_max
    own_kv = kv_src is None
    FRONT = ["x"] + ([] if own_kv else ["c"]) + ["q", "k", "v"]
    NFRONT = len(FRONT)
    at_front = {n: i + 1 for i, n in enumerate(FRONT)}
    NTAIL = 4
    HU = 1 if softmax_max else 2
    NS = H // HU
    NM = T * H // 2
    NNORM = 4 if use_mask else 2
    rows = ROWS + NPART if softmax_max else ROWS
    PACK = 16 * len(Q_PARTS)

    with ExitStack() as ctx:
        def sem(n):
            return ctx.enter_context(nc.semaphore(f"{name}_{n}"))

        x_in, c_in, r_in = sem("x_in"), sem("c_in"), sem("r_in")
        w_in, next_w_in = sem("w_in"), sem("next_w_in")
        front_full, front_free = sem("front_full"), sem("front_free")
        tail_full, tail_free = sem("tail_full"), sem("tail_free")
        scores_full, exp_done, clip_done = sem("scores_full"), sem("exp_done"), sem("clip_done")
        max_full, max_done = sem("max_full"), sem("max_done")
        max_parts, maxT_full, maxT_out, max_packed = (sem("max_parts"), sem("maxT_full"),
                                                      sem("maxT_out"), sem("max_packed"))
        acc_full, acc_out = sem("acc_full"), sem("acc_out")
        part_h, part_r, part_m, part_l = sem("part_h"), sem("part_r"), sem("part_m"), sem("part_l")
        q_stored, k_stored = sem("q_stored"), sem("k_stored")
        q_packed, k_packed = sem("q_packed"), sem("k_packed")
        norm_done = sem("norm_done")
        resid_ready = sem("resid_ready")
        y_done, var_done, rstd_done, xn_done, xo_done = (sem("y_done"), sem("var_done"),
                                                         sem("rstd_done"), sem("xn_done"), sem("xo_done"))
        x_stored = sem("x_stored")
        dve_norm, dve_max, dve_tail = sem("dve_norm"), sem("dve_max"), sem("dve_tail")
        pool_tail = sem("pool_tail")
        stats_seen, load_seen = sem("stats_seen"), sem("load_seen")
        block = ctx.enter_context(nc.Block())

        def tok(dram, b):
            return dram[bass.ds(b, 1)].rearrange("a (t p) d -> p (a t) d", p=P)

        @block.sync
        def _(sp):
            def load_inputs(b):
                sp.dma_start(m.xin[:], tok(q_src, b)).then_inc(x_in, 16)
                if not own_kv:
                    sp.dma_start(m.cin[:], tok(kv_src, b)).then_inc(c_in, 16)

            def pack(b, par, parts, dram, packed, groups, part_count, stored, packed_sem):
                reached(sp, load_seen, part_l, b * 2 + part_count)
                reached(sp, load_seen, packed_sem, b * PACK)
                sp.dma_start(dram.rearrange("t m p n -> p (t m) n"),
                             parts[:].rearrange("p t m n -> p (t m) n")).then_inc(stored, 16)
                reached(sp, load_seen, stored, b * 16 + 16)
                for g, part in enumerate(groups):
                    src = dram[part].rearrange("m (h d) n -> d (m h) n", d=DH)
                    sp.dma_start(packed[par][g * DH:(g + 1) * DH], src).then_inc(packed_sem, 16)

            def front(b, par, first):
                if not first:
                    reached(sp, load_seen, scores_full, b * NS - NS)
                pack(b, par, m.qs, m.q_dram, m.qp, Q_PARTS, 1, q_stored, q_packed)
                pack(b, par, m.ks, m.k_dram, m.kp, K_PARTS, 2, k_stored, k_packed)

            load_inputs(0)
            for tile, dram in w["now"]:
                sp.dma_start(tile, dram).then_inc(w_in, 16)
            reached(sp, load_seen, front_full, at_front["x" if own_kv else "c"])
            load_inputs(1)
            for tile, dram in loads:
                sp.dma_start(tile, dram).then_inc(next_w_in, 16)
            front(0, 0, True)

            def step(b, par, first, last):
                if softmax_max:
                    reached(sp, load_seen, maxT_out, b + 1)
                    if not first:
                        reached(sp, load_seen, scores_full, b * NS - NS)
                    for part in range(NPART):
                        sp.dma_start(m.qp[par][MAX_ROW + part:MAX_ROW + part + 1],
                                     m.maxT[part * H:(part + 1) * H]).then_inc(max_packed, 16)
                if not first:
                    reached(sp, load_seen, y_done, b)
                sp.dma_start(m.rin[:], tok(q_src, b)).then_inc(r_in, 16)
                if not last:
                    if first:
                        front(1, 1, True)
                    else:
                        front(b + 1, 1 - par, False)
                    if not isinstance(b, int) or b + 2 < B:
                        reached(sp, load_seen, front_full, (b + 1) * NFRONT + at_front["x" if own_kv else "c"])
                        load_inputs(b + 2)
                if not first:
                    reached(sp, load_seen, xo_done, b)
                    sp.dma_start(tok(x_out, b - 1), m.xo[:]).then_inc(x_stored, 16)

            over_batch(sp, step)
            reached(sp, load_seen, xo_done, B)
            sp.dma_start(tok(x_out, B - 1), m.xo[:]).then_inc(x_stored, 16)
            reached(sp, load_seen, x_stored, 16 * B)
            if loads:
                reached(sp, load_seen, next_w_in, 16 * len(loads))

        @block.tensor
        def _(pe):
            def mm(out, lhsT, rhs, k=0, n=1):
                return nc.tensor.matmul(out, lhsT, rhs, start=(k == 0), stop=(k == n - 1))

            def front_bank(b, job):
                after(pe, front_free, b * NFRONT + at_front[job] - 1)

            def transposes(b, job):
                src = m.xin if job == "x" else m.cin
                front_bank(b, job)
                pe.wait_ge(x_in if job == "x" else c_in, b * 16 + 16)
                for t in range(T):
                    for k in range(KT):
                        last = nc.tensor.transpose(m.ps_front[:, k * S + t * P:k * S + (t + 1) * P],
                                                   src[:, t, k * P:(k + 1) * P], m.ident_f[:])
                last.then_inc(front_full, 1)

            def project_qk(b, job):
                front_bank(b, job)
                srcT = m.xT if job == "q" or own_kv else m.cT
                for mt in range(KT):
                    for k in range(KT):
                        last = mm(m.ps_front[:, mt * S:(mt + 1) * S], w[job][:, k, mt * P:(mt + 1) * P],
                                  srcT[:, k, :], k, KT)
                last.then_inc(front_full, 1)

            def project_v(b):
                front_bank(b, "v")
                srcT = m.xT if own_kv else m.cT
                for t in range(T):
                    for k in range(KT):
                        last = mm(m.ps_front[:, t * D:(t + 1) * D], srcT[:, k, t * P:(t + 1) * P],
                                  w["v"][:, k, :], k, KT)
                last.then_inc(front_full, 1)

            def scores(b, par, u):
                if u == 0:
                    pe.wait_ge(q_packed, b * PACK + PACK)
                    pe.wait_ge(k_packed, b * PACK + PACK)
                    if softmax_max:
                        pe.wait_ge(max_packed, b * 48 + 48)
                after(pe, exp_done, b * NS + u - 1)
                for i in range(HU):
                    h = u * HU + i
                    bank = (u % 2) * HU + i
                    for kt in range(T):
                        last = mm(m.ps_scores[:, bank, kt * S:(kt + 1) * S],
                                  m.kp[par][0:rows, h, kt * P:(kt + 1) * P], m.qp[par][0:rows, h, :])
                last.then_inc(scores_full, 1)

            def max_scores(b, par, u):
                if u == 0:
                    pe.wait_ge(q_packed, b * PACK + PACK)
                    pe.wait_ge(k_packed, b * PACK + PACK)
                    after(pe, maxT_out, b)
                after(pe, max_done, b * NM + u - 1)
                t, h0 = u // (H // 2), 2 * (u % (H // 2))
                for i in range(2):
                    last = mm(m.ps_scores[:, 2 + u % 2, i * S:(i + 1) * S],
                              m.qp[par][0:ROWS, h0 + i, t * P:(t + 1) * P], m.kp[par][0:ROWS, h0 + i, :])
                last.then_inc(max_full, 1)

            def transpose_max(b):
                pe.wait_ge(max_parts, b + 1)
                out = m.ps_scores[:, 2, 0:P].bitcast(BF16)
                for t in range(T):
                    last = nc.tensor.transpose(out[:, t * P:(t + 1) * P],
                                               m.mparts[:, t].rearrange("p c h -> p (c h)"), m.ident_b[:])
                last.then_inc(maxT_full, 1)

            def attend(b, par, quad):
                if softmax_max:
                    pe.wait_ge(exp_done, b * NS + 4 * (quad + 1))
                else:
                    pe.wait_ge(clip_done, b * NS + 2 * (quad + 1))
                if quad == 0:
                    pe.wait_ge(front_free, b * NFRONT + at_front["v"])
                after(pe, acc_out, b * QUADS + quad - 1)
                for kt in range(T):
                    for j in range(4):
                        last = mm(m.ps_acc[32 * j:32 * j + 32, quad % 2, 0:S],
                                  m.vaug[par][:, kt, 4 * quad + j, :], m.probs[quad % 2][:, j, kt, :], kt, T)
                last.then_inc(acc_full, 1)

            def tail_bank(b, i):
                after(pe, tail_free, b * NTAIL + i)

            def context_rows(b, half):
                tail_bank(b, half)
                pe.wait_ge(acc_out, b * QUADS + 2 * half + 2)
                for t in range(T):
                    for q2 in range(2):
                        at = (t * 2 + q2) * P
                        last = nc.tensor.transpose(m.ps_tail[:, at:at + P],
                                                   m.acc[:, 2 * half + q2, t * P:(t + 1) * P], m.ident_f[:])
                last.then_inc(tail_full, 1)

            def context_back(b):
                tail_bank(b, 2)
                pe.wait_ge(norm_done, b * 2 + 2)
                for t in range(T):
                    for k in range(KT):
                        last = nc.tensor.transpose(m.ps_tail[:, k * S + t * P:k * S + (t + 1) * P],
                                                   m.ctx[:, t, k * P:(k + 1) * P], m.ident_f[:])
                last.then_inc(tail_full, 1)

            def project_out(b):
                tail_bank(b, 3)
                for t in range(T):
                    for k in range(KT):
                        last = mm(m.ps_tail[:, t * D:(t + 1) * D], m.ctxT[:, k, t * P:(t + 1) * P],
                                  w["o"][:, k, :], k, KT)
                last.then_inc(tail_full, 1)

            transposes(0, "x")
            if not own_kv:
                transposes(0, "c")
            if w["now"]:
                pe.wait_ge(w_in, 16 * len(w["now"]))
            project_qk(0, "q")
            project_qk(0, "k")
            project_v(0)
            if softmax_max:
                for u in range(NM):
                    max_scores(0, 0, u)

            def step_l0(b, par, first, last):
                nb, npar = b + 1, 1 - par
                if not first:
                    context_rows(b - 1, 1)
                if not last:
                    transposes(nb, "x")
                    transposes(nb, "c")
                transpose_max(b)
                if not last:
                    project_qk(nb, "q")
                if not first:
                    context_back(b - 1)
                if not last:
                    project_qk(nb, "k")
                scores(b, par, 0)
                scores(b, par, 1)
                if not last:
                    project_v(nb)
                scores(b, par, 2)
                scores(b, par, 3)
                if not first:
                    project_out(b - 1)
                attend(b, par, 0)
                scores(b, par, 4)
                scores(b, par, 5)
                u = 0
                for h in range(6, H):
                    if not last:
                        max_scores(nb, npar, u)
                        u += 1
                    scores(b, par, h)
                    if h % 4 == 3:
                        attend(b, par, h // 4)
                    if h == 9:
                        context_rows(b, 0)
                if not last:
                    while u < NM:
                        max_scores(nb, npar, u)
                        u += 1

            def step_l1(b, par, first, last):
                nb = b + 1
                scores(b, par, 0)
                scores(b, par, 1)
                if not first:
                    context_rows(b - 1, 1)
                if not last:
                    transposes(nb, "x")
                    if not own_kv:
                        transposes(nb, "c")
                scores(b, par, 2)
                attend(b, par, 0)
                if not first:
                    context_back(b - 1)
                scores(b, par, 3)
                if not last:
                    project_qk(nb, "q")
                scores(b, par, 4)
                if not first:
                    project_out(b - 1)
                attend(b, par, 1)
                if not last:
                    project_qk(nb, "k")
                scores(b, par, 5)
                scores(b, par, 6)
                if not last:
                    project_v(nb)
                attend(b, par, 2)
                context_rows(b, 0)
                scores(b, par, 7)
                attend(b, par, 3)

            over_batch(pe, step_l0 if softmax_max else step_l1)
            context_rows(B - 1, 1)
            context_back(B - 1)
            project_out(B - 1)

        @block.scalar
        def _(act):
            def evac_T(b, job):
                act.wait_ge(front_full, b * NFRONT + at_front[job])
                dst = m.xT if job == "x" else m.cT
                nc.scalar.copy(dst[:].rearrange("p k n -> p (k n)"), m.ps_front[:]).then_inc(front_free, 1)

            def high_part(b, job):
                parts, i = (m.qs, 0) if job == "q" else (m.ks, 1)
                act.wait_ge(front_full, b * NFRONT + at_front[job])
                after(act, q_stored if job == "q" else k_stored, b * 16)
                if has_bias:
                    for mt in range(KT):
                        last = nc.scalar.activation(parts[:, 0, mt, :], m.ps_front[:, mt * S:(mt + 1) * S],
                                                    ACT.Identity, bias=w["b" + job][:, mt:mt + 1])
                else:
                    last = nc.scalar.copy(parts[:, 0].rearrange("p m n -> p (m n)"), m.ps_front[:])
                last.then_inc(part_h, 1)

            def evac_v(b, par):
                act.wait_ge(front_full, b * NFRONT + at_front["v"])
                nc.scalar.copy(m.vaug[par][:, :, :, 0:DH],
                               m.ps_front[:].rearrange("p (t h d) -> p t h d", t=T, h=H)).then_inc(front_free, 1)

            def exp(b, u):
                act.wait_ge(scores_full, b * NS + u + 1)
                quad, at = u * HU // 4, u * HU % 4
                after(act, acc_full, b * QUADS + quad - 1)
                bank = (u % 2) * HU
                out = m.probs[quad % 2][:, at:at + HU].rearrange("p h t n -> p h (t n)")
                nc.scalar.activation(out, m.ps_scores[:, bank:bank + HU, :], ACT.Exp,
                                     scale=SCALE).then_inc(exp_done, 1)

            def evac_acc(b, quad):
                act.wait_ge(acc_full, b * QUADS + quad + 1)
                after(act, tail_full, b * NTAIL - NTAIL + 1 + quad // 2)
                nc.scalar.copy(m.acc[:, quad, :], m.ps_acc[:, quad % 2, 0:S]).then_inc(acc_out, 1)

            def evac_ctxT(b):
                act.wait_ge(tail_full, b * NTAIL + 3)
                nc.scalar.copy(m.ctxT[:].rearrange("p k n -> p (k n)"), m.ps_tail[:]).then_inc(tail_free, 1)

            def evac_maxT(b):
                act.wait_ge(maxT_full, b + 1)
                after(act, max_packed, b * 48)
                nc.scalar.copy(m.maxT[:], m.ps_scores[:, 2, 0:P].bitcast(BF16)[0:NPART * H, :]
                               ).then_inc(maxT_out, 1)

            evac_T(0, "x")
            if not own_kv:
                evac_T(0, "c")
            high_part(0, "q")
            high_part(0, "k")
            if not has_bias:
                evac_v(0, 0)

            def step_l0(b, par, first, last):
                if not last:
                    evac_T(b + 1, "x")
                    evac_T(b + 1, "c")
                evac_maxT(b)
                if not last:
                    high_part(b + 1, "q")
                if not first:
                    evac_ctxT(b - 1)
                if not last:
                    high_part(b + 1, "k")
                for quad in range(QUADS):
                    for u in range(4 * quad, 4 * quad + 4):
                        exp(b, u)
                    evac_acc(b, quad)

            def step_l1(b, par, first, last):
                exp(b, 0)
                exp(b, 1)
                if not last:
                    evac_T(b + 1, "x")
                    if not own_kv:
                        evac_T(b + 1, "c")
                exp(b, 2)
                evac_acc(b, 0)
                if not first:
                    evac_ctxT(b - 1)
                exp(b, 3)
                if not last:
                    high_part(b + 1, "q")
                exp(b, 4)
                evac_acc(b, 1)
                if not last:
                    high_part(b + 1, "k")
                exp(b, 5)
                exp(b, 6)
                if not last:
                    evac_v(b + 1, 1 - par)
                evac_acc(b, 2)
                exp(b, 7)
                evac_acc(b, 3)

            over_batch(act, step_l0 if softmax_max else step_l1)
            evac_ctxT(B - 1)

        @block.vector
        def _(dve):
            norm = Chain(dve, dve_norm, 2 * NNORM)
            tail = Chain(dve, dve_tail, 2)
            maxc = Chain(dve, dve_max, 3)

            def lower_parts(b, job):
                parts, i = (m.qs, 0) if job == "q" else (m.ks, 1)
                dve.wait_ge(part_h, b * 2 + i + 1)
                after(dve, part_l, (b - 1) * 2 + 1 + i)
                after(dve, q_stored if job == "q" else k_stored, b * 16)
                if has_bias:
                    for mt in range(KT):
                        last = nc.vector.scalar_tensor_tensor(
                            m.rest[i][:, mt, :], m.ps_front[:, mt * S:(mt + 1) * S], w["b" + job][:, mt:mt + 1],
                            parts[:, 0, mt, :], ALU.add, ALU.subtract)
                        if mt < KT - 1:
                            continue
                        last.then_inc(part_r, 1)
                else:
                    nc.vector.tensor_tensor(m.rest[i][:].rearrange("p m n -> p (m n)"), m.ps_front[:],
                                            parts[:, 0].rearrange("p m n -> p (m n)"),
                                            ALU.subtract).then_inc(part_r, 1)
                dve.wait_ge(part_r, b * 2 + i + 1)
                dve.sem_inc(front_free, 1)
                nc.vector.tensor_copy(parts[:, 1], m.rest[i][:]).then_inc(part_m, 1)

            def evac_v(b, par):
                dve.wait_ge(front_full, b * NFRONT + at_front["v"])
                nc.vector.tensor_tensor(
                    m.vaug[par][:, :, :, 0:DH], m.ps_front[:].rearrange("p (t h d) -> p t h d", t=T, h=H),
                    w["bv"][:].rearrange("p t (h d) -> p t h d", h=H), ALU.add).then_inc(front_free, 1)

            def row_max(b, u):
                dve.wait_ge(max_full, b * NM + u + 1)
                if u == 0:
                    after(dve, max_parts, b)
                t, h0 = u // (H // 2), 2 * (u % (H // 2))
                nc.vector.reduce_max(m.rmax[:, t, h0:h0 + 2],
                                     m.ps_scores[:, 2 + u % 2, :].rearrange("p (h n) -> p h n", h=2),
                                     AX_X).then_inc(max_done, 1)

            def split_max(b):
                maxc.start(b)
                dve.wait_ge(max_done, b * NM + NM)
                after(dve, maxT_full, b)
                hp, mp, lp = (m.mparts[:, :, c, :] for c in range(NPART))
                maxc.link(nc.vector.tensor_scalar(hp, m.rmax[:], -1.0, None, ALU.mult))
                maxc.link(nc.vector.scalar_tensor_tensor(m.rrest[:], m.rmax[:], -1.0, hp, ALU.mult, ALU.subtract))
                maxc.link(nc.vector.tensor_copy(mp, m.rrest[:]))
                nc.vector.tensor_tensor(lp, m.rrest[:], mp, ALU.subtract).then_inc(max_parts, 1)
                maxc.end()

            def clip(b, u):
                dve.wait_ge(exp_done, b * NS + u + 1)
                quad, at = u // 2, 2 * (u % 2)
                p = m.probs[quad % 2][:, at:at + 2].rearrange("p h t n -> p (h t n)")
                nc.vector.tensor_scalar(p, p, CLIP_LO, CLIP_HI, ALU.max, ALU.min).then_inc(clip_done, 1)

            def normalise(b, half):
                norm.start(b, half * NNORM)
                dve.wait_ge(tail_full, b * NTAIL + half + 1)
                if half == 0:
                    after(dve, tail_full, (b - 1) * NTAIL + 3)
                rowsT = m.ps_tail[:].rearrange("p (t h c) -> p t h c", t=T, c=32)
                den = rowsT[:, :, :, DH]
                shape = (P, T, H // 2)
                if use_mask:
                    keep = m.maskf[:, bass.ds(b, 1), :].rearrange("p a t -> p (a t)")
                    keep = keep.rearrange("p (t o) -> p t o", o=1).to_broadcast(shape)
                    norm.link(nc.vector.tensor_tensor(m.den[:], den, keep, ALU.mult))
                    norm.link(nc.vector.scalar_tensor_tensor(m.den2[:], m.den[:], 0.0, m.den[:],
                                                             ALU.is_le, ALU.add))
                    norm.link(nc.vector.reciprocal(m.rden[:], m.den2[:]))
                    norm.link(nc.vector.tensor_tensor(m.rden2[:], m.rden[:], keep, ALU.mult))
                    rden = m.rden2
                else:
                    norm.link(nc.vector.tensor_copy(m.den[:], den))
                    norm.link(nc.vector.reciprocal(m.rden[:], m.den[:]))
                    rden = m.rden
                out = m.ctx[:, :, half * P:(half + 1) * P].rearrange("p t (h d) -> p t h d", d=DH)
                nc.vector.tensor_tensor(
                    out, rowsT[:, :, :, 0:DH],
                    rden[:].rearrange("p t (h o) -> p t h o", o=1).to_broadcast((P, T, H // 2, DH)),
                    ALU.mult).then_inc(norm_done, 1)
                dve.wait_ge(norm_done, b * 2 + half + 1)
                dve.sem_inc(tail_free, 1)
                if half == 1:
                    norm.end()

            def add_and_stats(b):
                tail.start(b)
                dve.wait_ge(tail_full, b * NTAIL + 4)
                if has_bias:
                    dve.wait_ge(resid_ready, b + 1)
                else:
                    dve.wait_ge(r_in, b * 16 + 16)
                after(dve, xn_done, b)
                nc.vector.tensor_tensor(m.y[:].rearrange("p t d -> p (t d)"), m.ps_tail[:],
                                        m.rin[:].rearrange("p t d -> p (t d)"), ALU.add).then_inc(y_done, 1)
                dve.wait_ge(y_done, b + 1)
                dve.sem_inc(tail_free, 1)
                nc.vector.bn_stats(m.stats[:, 0, :], m.y[:, 0, :])
                tail.link(nc.vector.bn_stats(m.stats[:, 1, :], m.y[:, 1, :]))
                dve.sem_inc(stats_seen, 1)
                nc.vector.bn_aggr(m.mv[:, 0, :], m.stats[:, 0, :])
                tail.link(nc.vector.bn_aggr(m.mv[:, 1, :], m.stats[:, 1, :]))
                dve.sem_inc(var_done, 1)
                tail.end()

            def scale_rows(b):
                dve.wait_ge(rstd_done, b + 1)
                after(dve, xo_done, b)
                for t in range(T):
                    last = nc.vector.tensor_scalar(m.xn[:, t, :], m.y[:, t, :], m.mv[:, t, 0:1],
                                                   m.rstd[:, t:t + 1], ALU.subtract, ALU.mult)
                last.then_inc(xn_done, 1)

            lower_parts(0, "q")
            lower_parts(0, "k")
            if has_bias:
                dve.wait_ge(w_in, 16 * len(w["now"]))
                evac_v(0, 0)
            if softmax_max:
                for u in range(NM):
                    row_max(0, u)
                split_max(0)

            def step_l0(b, par, first, last):
                if not first:
                    normalise(b - 1, 1)
                if not last:
                    lower_parts(b + 1, "q")
                    lower_parts(b + 1, "k")
                    evac_v(b + 1, 1 - par)
                if not first:
                    add_and_stats(b - 1)
                    if last:
                        scale_rows(b - 1)
                if not last:
                    for u in range(2):
                        row_max(b + 1, u)
                    if not first:
                        scale_rows(b - 1)
                    for u in range(2, 4):
                        row_max(b + 1, u)
                normalise(b, 0)
                if not last:
                    for u in range(4, NM):
                        row_max(b + 1, u)
                    split_max(b + 1)

            def step_l1(b, par, first, last):
                clip(b, 0)
                clip(b, 1)
                if not first:
                    normalise(b - 1, 1)
                clip(b, 2)
                clip(b, 3)
                if not last:
                    lower_parts(b + 1, "q")
                clip(b, 4)
                if not first:
                    add_and_stats(b - 1)
                if not last:
                    lower_parts(b + 1, "k")
                clip(b, 5)
                if not first:
                    scale_rows(b - 1)
                clip(b, 6)
                normalise(b, 0)
                clip(b, 7)

            over_batch(dve, step_l0 if softmax_max else step_l1)
            normalise(B - 1, 1)
            add_and_stats(B - 1)
            scale_rows(B - 1)

        @block.gpsimd
        def _(pool):
            tail = Chain(pool, pool_tail, 2)

            def low_part(b, job):
                parts, i = (m.qs, 0) if job == "q" else (m.ks, 1)
                pool.wait_ge(part_m, b * 2 + i + 1)
                nc.gpsimd.tensor_tensor(parts[:, 2], m.rest[i][:], parts[:, 1], ALU.subtract).then_inc(part_l, 1)

            def rstd(b):
                tail.start(b)
                pool.wait_ge(var_done, b + 1)
                tail.link(nc.gpsimd.tensor_tensor(m.vare[:], m.mv[:, :, 1], m.eps[eps][:, 0:T], ALU.add))
                nc.gpsimd.tensor_tensor(m.rstd[:], m.vare[:], m.neg_half[:, 0:T], ALU.pow).then_inc(rstd_done, 1)

            def affine(b):
                pool.wait_ge(xn_done, b + 1)
                tail.link(nc.gpsimd.tensor_tensor(m.xg[:], m.xn[:], w["gamma"][:], ALU.mult))
                after(pool, x_stored, b * 16)
                nc.gpsimd.tensor_tensor(m.xo[:], m.xg[:], w["beta"][:], ALU.add).then_inc(xo_done, 1)
                tail.end()

            def residual(b):
                pool.wait_ge(r_in, b * 16 + 16)
                nc.gpsimd.tensor_tensor(m.rin[:], m.rin[:], w["bo"][:], ALU.add).then_inc(resid_ready, 1)

            if w["now"]:
                pool.wait_ge(w_in, 16 * len(w["now"]))
            low_part(0, "q")
            low_part(0, "k")

            def step(b, par, first, last):
                if not last:
                    low_part(b + 1, "q")
                if softmax_max and not last:
                    low_part(b + 1, "k")
                if not first:
                    rstd(b - 1)
                if not softmax_max and not last:
                    low_part(b + 1, "k")
                if not first:
                    affine(b - 1)
                if has_bias:
                    residual(b)

            over_batch(pool, step)
            rstd(B - 1)
            affine(B - 1)


def ffn_phase(nc, m, x_src, out, w):
    PAIR = 2
    NT = PAIR * T
    N = PAIR * S
    FT = FF // P
    with ExitStack() as ctx:
        def sem(n):
            return ctx.enter_context(nc.semaphore(f"ffn_{n}"))

        x_in, xT_full, xT_out = sem("x_in"), sem("xT_full"), sem("xT_out")
        up_full, gelu_done = sem("up_full"), sem("gelu_done")
        down_full, y_done = sem("down_full"), sem("y_done")
        resid_ready, stats_done, var_done = sem("resid_ready"), sem("stats_done"), sem("var_done")
        vare_done, rstd_done, xn_done = sem("vare_done"), sem("rstd_done"), sem("xn_done")
        xg_done, xo_done, stored = sem("xg_done"), sem("xo_done"), sem("stored")
        stats_seen, load_seen = sem("stats_seen"), sem("load_seen")
        block = ctx.enter_context(nc.Block())
        NSTEP = B // PAIR

        def tok(dram, i):
            return dram[bass.ds(i * PAIR, PAIR)].rearrange("a (t p) d -> p (a t) d", p=P)

        @block.sync
        def _(sp):
            sp.dma_start(m.f_x[:], tok(x_src, 0)).then_inc(x_in, 16)

            def store(i):
                reached(sp, load_seen, xo_done, i + 1)
                sp.dma_start(tok(out, i), m.f_xo[:]).then_inc(stored, 16)

            with sp.Fori(0, NSTEP - 1) as i:
                reached(sp, load_seen, y_done, i * NT + NT)
                sp.dma_start(m.f_x[:], tok(x_src, i + 1)).then_inc(x_in, 16)
                store(i)
            store(NSTEP - 1)
            reached(sp, load_seen, stored, 16 * NSTEP)

        @block.tensor
        def _(pe):
            def step(i, first):
                pe.wait_ge(x_in, i * 16 + 16)
                for a in range(PAIR):
                    if not first:
                        pe.wait_ge(xT_out, i * PAIR)
                    for t in range(T):
                        for k in range(KT):
                            last = nc.tensor.transpose(m.ps_scores[:, a, k * S + t * P:k * S + (t + 1) * P],
                                                       m.f_x[:, a * T + t, k * P:(k + 1) * P], m.ident_f[:])
                    last.then_inc(xT_full, 1)
                pe.wait_ge(xT_out, i * PAIR + PAIR)
                for f in range(FT):
                    if not (first and f < 2):
                        pe.wait_ge(gelu_done, i * FT + f - 1)
                    for k in range(KT):
                        last = nc.tensor.matmul(m.ps_scores[:, 2 + f % 2, :], w["w1"][:, k, f * P:(f + 1) * P],
                                                m.f_xT[:, k, :], start=(k == 0), stop=(k == KT - 1))
                    last.then_inc(up_full, 1)
                for t in range(NT):
                    if not (first and t < 2):
                        pe.wait_ge(y_done, i * NT + t - 1)
                    for f in range(FT):
                        if t == 0:
                            pe.wait_ge(gelu_done, i * FT + f + 1)
                        last = nc.tensor.matmul(m.ps_acc[:, t % 2, 0:D], m.f_h[:, f, t * P:(t + 1) * P],
                                                w["w2"][:, f, :], start=(f == 0), stop=(f == FT - 1))
                    last.then_inc(down_full, 1)

            step(0, True)
            with pe.Fori(1, NSTEP) as i:
                step(i, False)

        @block.scalar
        def _(act):
            def step(i, first):
                for a in range(PAIR):
                    act.wait_ge(xT_full, i * PAIR + a + 1)
                    nc.scalar.copy(m.f_xT[:, :, a * S:(a + 1) * S],
                                   m.ps_scores[:, a, :].rearrange("p (k n) -> p k n", k=KT)).then_inc(xT_out, 1)
                for f in range(FT):
                    act.wait_ge(up_full, i * FT + f + 1)
                    if not first:
                        act.wait_ge(down_full, i * NT)
                    nc.scalar.activation(m.f_h[:, f, :], m.ps_scores[:, 2 + f % 2, :], ACT.Gelu,
                                         bias=w["b1"][:, f:f + 1]).then_inc(gelu_done, 1)

            step(0, True)
            with act.Fori(1, NSTEP) as i:
                step(i, False)

        @block.vector
        def _(dve):
            def step(i, first):
                dve.wait_ge(resid_ready, i + 1)
                if not first:
                    dve.wait_ge(xn_done, i)
                for t in range(NT):
                    dve.wait_ge(down_full, i * NT + t + 1)
                    nc.vector.tensor_tensor(m.f_y[:, t, :], m.ps_acc[:, t % 2, 0:D], m.f_r[:, t, :],
                                            ALU.add).then_inc(y_done, 1)
                    dve.wait_ge(y_done, i * NT + t + 1)
                    nc.vector.bn_stats(m.f_stats[:, t, :], m.f_y[:, t, :]).then_inc(stats_done, 1)
                    dve.wait_ge(stats_done, i * NT + t + 1)
                    dve.sem_inc(stats_seen, 1)
                    nc.vector.bn_aggr(m.f_mv[:, t, :], m.f_stats[:, t, :]).then_inc(var_done, 1)
                dve.wait_ge(rstd_done, i + 1)
                if not first:
                    dve.wait_ge(xg_done, i)
                for t in range(NT):
                    last = nc.vector.tensor_scalar(m.f_xn[:, t, :], m.f_y[:, t, :], m.f_mv[:, t, 0:1],
                                                   m.f_rstd[:, t:t + 1], ALU.subtract, ALU.mult)
                last.then_inc(xn_done, 1)

            step(0, True)
            with dve.Fori(1, NSTEP) as i:
                step(i, False)

        @block.gpsimd
        def _(pool):
            def step(i, first):
                pool.wait_ge(x_in, i * 16 + 16)
                if not first:
                    pool.wait_ge(y_done, i * NT)
                for a in range(PAIR):
                    last = nc.gpsimd.tensor_tensor(m.f_r[:, a * T:(a + 1) * T], m.f_x[:, a * T:(a + 1) * T],
                                                   w["b2"][:], ALU.add)
                last.then_inc(resid_ready, 1)
                pool.wait_ge(var_done, i * NT + NT)
                nc.gpsimd.tensor_tensor(m.f_vare[:], m.f_mv[:, :, 1], m.eps[1e-5][:],
                                        ALU.add).then_inc(vare_done, 1)
                pool.wait_ge(vare_done, i + 1)
                nc.gpsimd.tensor_tensor(m.f_rstd[:], m.f_vare[:], m.neg_half[:], ALU.pow).then_inc(rstd_done, 1)
                pool.wait_ge(xn_done, i + 1)
                for a in range(PAIR):
                    last = nc.gpsimd.tensor_tensor(m.f_xg[:, a * T:(a + 1) * T], m.f_xn[:, a * T:(a + 1) * T],
                                                   w["gamma"][:], ALU.mult)
                last.then_inc(xg_done, 1)
                pool.wait_ge(xg_done, i + 1)
                if not first:
                    pool.wait_ge(stored, i * 16)
                for a in range(PAIR):
                    last = nc.gpsimd.tensor_tensor(m.f_xo[:, a * T:(a + 1) * T], m.f_xg[:, a * T:(a + 1) * T],
                                                   w["beta"][:], ALU.add)
                last.then_inc(xo_done, 1)

            step(0, True)
            with pool.Fori(1, NSTEP) as i:
                step(i, False)


class Memory:
    pass


def build(nc, a, out):
    with ExitStack() as ctx:
        def sb(name, shape, dt=F32):
            return ctx.enter_context(nc.sbuf_tensor(name, shape, dt))

        def pair(name, shape, dt):
            return [sb(f"{name}{i}", shape, dt) for i in range(2)]

        m = Memory()
        m.ident_f, m.ident_b = sb("ident_f", [P, P]), sb("ident_b", [P, P], BF16)
        m.mask_u8, m.maskf = sb("mask_u8", [P, B, T], U8), sb("maskf", [P, B, T])
        m.neg_half = sb("neg_half", [P, 2 * T])
        m.eps = {1e-6: sb("eps_l0", [P, 2 * T]), 1e-5: sb("eps_l1", [P, 2 * T])}
        m.xin, m.cin, m.rin = sb("xin", [P, T, D]), sb("cin", [P, T, D]), sb("rin", [P, T, D])
        m.xT, m.cT = sb("xT", [P, KT, S]), sb("cT", [P, KT, S])
        m.qs, m.ks = sb("q_parts", [P, NPART, KT, S], BF16), sb("k_parts", [P, NPART, KT, S], BF16)
        m.rest = pair("rest", [P, KT, S], F32)
        m.qp, m.kp = pair("q_packed", [P, H, S], BF16), pair("k_packed", [P, H, S], BF16)
        m.vaug = pair("v_ones", [P, T, H, 32], F32)
        m.probs = pair("probs", [P, 4, T, S], F32)
        m.acc = sb("acc", [P, QUADS, S])
        m.rmax, m.rrest = sb("rmax", [P, T, H]), sb("rmax_rest", [P, T, H])
        m.mparts, m.maxT = sb("max_parts", [P, T, P // H, H], BF16), sb("maxT", [NPART * H, S], BF16)
        m.den, m.den2, m.rden, m.rden2 = (sb(n, [P, T, H // 2]) for n in ("den", "den2", "rden", "rden2"))
        m.ctx, m.ctxT = sb("ctx", [P, T, D]), sb("ctxT", [P, KT, S])
        m.y, m.xn, m.xg, m.xo = (sb(n, [P, T, D]) for n in ("y", "xn", "xg", "xo"))
        m.stats, m.mv = sb("stats", [P, T, 6]), sb("mv", [P, T, 2])
        m.vare, m.rstd = sb("vare", [P, T]), sb("rstd", [P, T])
        m.f_x, m.f_r, m.f_y, m.f_xn, m.f_xg, m.f_xo = (
            sb(f"f_{n}", [P, 2 * T, D]) for n in ("x", "r", "y", "xn", "xg", "xo"))
        m.f_xT, m.f_h = sb("f_xT", [P, KT, 2 * S]), sb("f_h", [P, FF // P, 2 * S])
        m.f_stats, m.f_mv = sb("f_stats", [P, 2 * T, 6]), sb("f_mv", [P, 2 * T, 2])
        m.f_vare, m.f_rstd = sb("f_vare", [P, 2 * T]), sb("f_rstd", [P, 2 * T])
        m.ps_scores = ctx.enter_context(nc.psum_tensor("ps_scores", [P, 4, 512], F32))
        m.ps_acc = ctx.enter_context(nc.psum_tensor("ps_acc", [P, 2, 512], F32))
        m.ps_front = ctx.enter_context(nc.psum_tensor("ps_front", [P, 512], F32))
        m.ps_tail = ctx.enter_context(nc.psum_tensor("ps_tail", [P, 512], F32))
        m.q_dram = nc.dram_tensor("q_scratch", (NPART, KT, P, S), BF16, kind="Internal").ap()
        m.k_dram = nc.dram_tensor("k_scratch", (NPART, KT, P, S), BF16, kind="Internal").ap()
        x1 = nc.dram_tensor("x_after_l0", (B, S, D), F32, kind="Internal").ap()
        x2 = nc.dram_tensor("x_after_self", (B, S, D), F32, kind="Internal").ap()
        x3 = nc.dram_tensor("x_after_cross", (B, S, D), F32, kind="Internal").ap()

        def mat(name, dram):
            n = dram.shape[1]
            t = sb(name, [P, dram.shape[0] // P, n])
            return t, (t[:], dram.rearrange("(k p) n -> p k n", p=P))

        def cols(name, vec):
            t = sb(name, [P, vec.shape[0] // P])
            return t, (t[:], vec.rearrange("(m p) -> p m", p=P))

        def row(name, vec):
            t = sb(name, [P, T, D])
            src = vec.rearrange("(o d) -> o d", o=1).to_broadcast((P, D))
            return t, [(t[:, i, :], src) for i in range(T)]

        def weights(prefix, names, kind_cols=(), kind_rows=()):
            w, loads = {}, []
            for key, name in names:
                w[key], load = mat(f"{prefix}_{key}", a[name])
                loads.append(load)
            for key, name in kind_cols:
                w[key], load = cols(f"{prefix}_{key}", a[name])
                loads.append(load)
            for key, name in kind_rows:
                w[key], ls = row(f"{prefix}_{key}", a[name])
                loads += ls
            return w, loads

        w0, l0 = weights("l0", [("q", "L0_xattn_Wq"), ("k", "L0_xattn_Wk"), ("v", "L0_xattn_Wv"), ("o", "L0_xattn_Wo")],
                         [("bq", "L0_xattn_bq"), ("bk", "L0_xattn_bk")],
                         [("bv", "L0_xattn_bv"), ("bo", "L0_xattn_bo"),
                          ("gamma", "L0_xattn_gamma"), ("beta", "L0_xattn_beta")])
        ws, ls = weights("sa", [(k, f"L1_xattn_sa_w{k}") for k in "qkvo"], (),
                         [("gamma", "L1_xattn_g1"), ("beta", "L1_xattn_be1")])
        wc, lc = weights("ca", [(k, f"L1_xattn_ca_w{k}") for k in "qkvo"], (),
                         [("gamma", "L1_xattn_g2"), ("beta", "L1_xattn_be2")])
        wf, lf = weights("ff", [("w1", "L1_xattn_w1"), ("w2", "L1_xattn_w2")], [("b1", "L1_xattn_b1")],
                         [("b2", "L1_xattn_b2"), ("gamma", "L1_xattn_g3"), ("beta", "L1_xattn_be3")])
        w0["now"], ws["now"], wc["now"] = l0, [], []

        ctx.enter_context(nc.allow_non_contiguous_dma(reason="biases and the mask are laid out once"))
        setup(nc, m, a["mask_BxS_bf1"], m.ident_f, m.ident_b)
        attention_phase(nc, m, "l0", a["x"], a["ctx_1024"], x1, w0, True, False, 1e-6, ls + lc + lf)
        attention_phase(nc, m, "sa", x1, None, x2, ws, False, True, 1e-5, [])
        attention_phase(nc, m, "ca", x2, a["ctx_1024"], x3, wc, False, False, 1e-5, [])
        ffn_phase(nc, m, x3, out, wf)


_INS = ["x", "ctx_1024", "mask_BxS_bf1",
        "L0_xattn_Wv", "L0_xattn_bv", "L0_xattn_Wk", "L0_xattn_bk", "L0_xattn_Wq", "L0_xattn_bq",
        "L0_xattn_Wo", "L0_xattn_bo", "L0_xattn_gamma", "L0_xattn_beta",
        "L1_xattn_sa_wq", "L1_xattn_sa_wk", "L1_xattn_sa_wv", "L1_xattn_sa_wo",
        "L1_xattn_ca_wq", "L1_xattn_ca_wk", "L1_xattn_ca_wv", "L1_xattn_ca_wo",
        "L1_xattn_w1", "L1_xattn_b1", "L1_xattn_w2", "L1_xattn_b2",
        "L1_xattn_g1", "L1_xattn_be1", "L1_xattn_g2", "L1_xattn_be2", "L1_xattn_g3", "L1_xattn_be3"]


def kernel(**inputs):
    import numpy as _np
    import concourse.bacc as _bacc
    from concourse import mybir as _mybir
    from concourse.bass_utils import run_bass_kernel_spmd as _run

    nc = _bacc.Bacc("TRN2", target_bir_lowering=False, num_devices=1)
    arrays, args = {}, {}
    for name in _INS:
        v = _np.ascontiguousarray(inputs[name])
        if v.dtype == _np.bool_:
            v = v.view(_np.uint8)
        arrays[f"in_{name}"] = v
        args[name] = nc.dram_tensor(f"in_{name}", v.shape, _mybir.dt.from_np(v.dtype), kind="ExternalInput").ap()
    out = nc.dram_tensor("out_0", (B, S, D), F32, kind="ExternalOutput").ap()
    build(nc, args, out)
    r = _run(nc, [arrays], core_ids=[0])
    return r.results[0]["out_0"]
```

```python
from contextlib import ExitStack

import numpy as np

import concourse.bass as bass
from concourse import mybir

F32 = mybir.dt.float32
BF16 = mybir.dt.bfloat16
U8 = mybir.dt.uint8
ACT = mybir.ActivationFunctionType
ALU = mybir.AluOpType
AX_X = mybir.AxisListType.X

P = 128
B, S, D = 8, 256, 256
H = 16
DH = D // H
FF = 4 * D
T = S // P
KT = D // P
SCALE = float(DH) ** -0.5
Q_PARTS = (0, 0, 0, 1, 1, 2)
K_PARTS = (0, 1, 2, 0, 1, 0)
ROWS = DH * len(Q_PARTS)
MAX_ROW = ROWS
NPART = 3
QUADS = H // 4
CLIP_LO, CLIP_HI = float(np.exp(np.float32(-50.0))), float(np.exp(np.float32(50.0)))


def over_batch(engine, step, loop_from=2):
    for b in range(loop_from):
        step(b, b % 2, b == 0, False)
    with engine.Fori(0, (B - 4) // 2) as pair:
        for j in range(2):
            step(pair * 2 + (loop_from + j), (loop_from + j) % 2, False, False)
    for b in range(loop_from + B - 4, B):
        step(b, b % 2, False, b == B - 1)


def after(engine, sem, value):
    if not isinstance(value, int) or value > 0:
        engine.wait_ge(sem, value)


def reached(engine, seen, sem, value):
    if not isinstance(value, int) or value > 0:
        engine.wait_ge(sem, value)
        engine.sem_inc(seen, 1)


class Chain:

    def __init__(self, engine, sem):
        self.engine, self.sem = engine, sem

    def start(self, done):
        self.done = done

    def link(self, ins):
        self.done = self.done + 1
        ins.then_inc(self.sem, 1)
        self.engine.wait_ge(self.sem, self.done)


class Attention:

    def __init__(self, prev, name, q_src, kv_src, out, w, l0=False, masked=False, eps=1e-5):
        self.name, self.q_src, self.kv_src, self.out, self.w = name, q_src, kv_src, out, w
        self.l0 = l0
        self.masked, self.eps = masked, eps
        self.own_kv = kv_src is None
        self.prev, self.next = prev, None
        self.jobs = ["x"] + ([] if self.own_kv else ["c"]) + ["q", "k", "v"]
        self.last_T = "x" if self.own_kv else "c"
        self.heads = 1 if l0 else 2
        self.units = H // self.heads
        self.norm_steps = 4 if masked else 2
        self.ahead = 2 if l0 else 1
        if prev is None:
            self.g0 = self.front0 = self.scores0 = self.norm0 = self.c0 = self.clip0 = 0
        else:
            prev.next = self
            self.g0 = prev.g(B)
            self.front0, self.scores0 = prev.front(B), prev.scores(B)
            self.norm0, self.c0, self.clip0 = prev.norm(B), prev.c(B), prev.clip(B)

    def g(self, b):
        return b + self.g0

    def front(self, b):
        return b * len(self.jobs) + self.front0

    def at(self, b, job):
        return self.front(b) + self.jobs.index(job) + 1

    def scores(self, b):
        return b * self.units + self.scores0

    def clip(self, b):
        return b * (0 if self.l0 else self.units) + self.clip0

    def c(self, b):
        return b * (0 if self.own_kv else 1) + self.c0

    def norm(self, b):
        return b * (2 * self.norm_steps) + self.norm0


def attention(nc, m, phases, now, later, ffn):
    L0 = phases[0]
    NTAIL = 4
    NM = T * H // 2
    PACK = 16 * len(Q_PARTS)
    MAXROWS = 16 * NPART

    with ExitStack() as ctx:
        def sem(n):
            return ctx.enter_context(nc.semaphore(n))

        x_in, c_in, r_in = sem("x_in"), sem("c_in"), sem("r_in")
        now_in, later_in, mask_in = sem("now_in"), sem("later_in"), sem("mask_in")
        ident_filled, ident_ready = sem("ident_filled"), sem("ident_ready")
        consts_ready, ones_ready, mask_ready = sem("consts_ready"), sem("ones_ready"), sem("mask_ready")
        front_full, front_free = sem("front_full"), sem("front_free")
        tail_full, tail_free = sem("tail_full"), sem("tail_free")
        scores_full, exp_done, clip_done = sem("scores_full"), sem("exp_done"), sem("clip_done")
        max_full, max_done, max_parts = sem("max_full"), sem("max_done"), sem("max_parts")
        maxT_full, maxT_out, max_packed = sem("maxT_full"), sem("maxT_out"), sem("max_packed")
        acc_full, acc_out = sem("acc_full"), sem("acc_out")
        part_h, part_r, part_m, part_l = sem("part_h"), sem("part_r"), sem("part_m"), sem("part_l")
        q_stored, k_stored = sem("q_stored"), sem("k_stored")
        q_packed, k_packed = sem("q_packed"), sem("k_packed")
        norm_done, resid_ready = sem("norm_done"), sem("resid_ready")
        y_done, var_done, rstd_done = sem("y_done"), sem("var_done"), sem("rstd_done")
        xn_done, xo_done, x_stored = sem("xn_done"), sem("xo_done"), sem("x_stored")
        dve_norm, dve_max, dve_tail, pool_tail = (sem("dve_norm"), sem("dve_max"), sem("dve_tail"),
                                                  sem("pool_tail"))
        stats_seen, load_seen = sem("stats_seen"), sem("load_seen")
        ffn.semaphores(sem)
        block = ctx.enter_context(nc.Block())

        def tok(dram, b):
            return dram[bass.ds(b, 1)].rearrange("a (t p) d -> p (a t) d", p=P)

        def front_target(ph, b, last):
            if last:
                return (ph.next, 0) if ph.next else None
            if ph.l0 and isinstance(b, int) and b + 2 >= B:
                return None
            return ph, b + ph.ahead

        def target_parity(ph, par, last):
            if last:
                return 0
            return par if ph.l0 else 1 - par

        def tail_target(ph, b, first):
            if first:
                return (ph.prev, B - 1) if ph.prev else None
            return ph, b - 1

        @block.sync
        def _(sp):
            def load_inputs(ph, b):
                if ph.prev:
                    after(sp, x_stored, ph.prev.g(b) * 16 + 16)
                    sp.sem_inc(load_seen, 1)
                sp.dma_start(m.xin[:], tok(ph.q_src, b)).then_inc(x_in, 16)
                if not ph.own_kv:
                    sp.dma_start(m.cin[:], tok(ph.kv_src, b)).then_inc(c_in, 16)

            def store_parts(ph, b, parts, dram, count, stored, packed_sem):
                reached(sp, load_seen, part_l, ph.g(b) * 2 + count)
                reached(sp, load_seen, packed_sem, ph.g(b) * PACK)
                sp.dma_start(dram.rearrange("t m p n -> p (t m) n"),
                             parts[:].rearrange("p t m n -> p (t m) n")).then_inc(stored, 16)

            def fetch_packed(ph, b, par, dram, packed, groups, stored, packed_sem):
                reached(sp, load_seen, stored, ph.g(b) * 16 + 16)
                for g, part in enumerate(groups):
                    src = dram[part].rearrange("m (h d) n -> d (m h) n", d=DH)
                    sp.dma_start(packed[par][g * DH:(g + 1) * DH], src).then_inc(packed_sem, 16)

            def store_q_k(ph, b):
                store_parts(ph, b, m.qs, m.q_dram, 1, q_stored, q_packed)
                store_parts(ph, b, m.ks, m.k_dram, 2, k_stored, k_packed)

            def fetch_q_k(ph, b, par):
                fetch_packed(ph, b, par, m.q_dram, m.qp, Q_PARTS, q_stored, q_packed)
                fetch_packed(ph, b, par, m.k_dram, m.kp, K_PARTS, k_stored, k_packed)

            def load_residual(ph, b):
                reached(sp, load_seen, y_done, ph.g(b))
                sp.dma_start(m.rin[:], tok(ph.q_src, b)).then_inc(r_in, 16)

            def store_x(ph, b):
                reached(sp, load_seen, xo_done, ph.g(b) + 1)
                sp.dma_start(tok(ph.out, b), m.xo[:]).then_inc(x_stored, 16)

            load_inputs(L0, 0)
            for tile, dram in now:
                sp.dma_start(tile, dram).then_inc(now_in, 16)
            sp.dma_start(*m.mask_load).then_inc(mask_in, 16)
            reached(sp, load_seen, front_full, L0.at(0, "c"))
            load_inputs(L0, 1)
            for tile, dram in later:
                sp.dma_start(tile, dram).then_inc(later_in, 16)
            for b in range(2):
                store_q_k(L0, b)
                fetch_q_k(L0, b, b)

            def step_l0(ph, b, par, first, last):
                front = front_target(ph, b, last)
                if front:
                    reached(sp, load_seen, front_full, ph.at(B - 1 if last else b + 1, "c"))
                    load_inputs(*front)
                reached(sp, load_seen, maxT_out, b + 1)
                for part in range(NPART):
                    sp.dma_start(m.qp[par][MAX_ROW + part:MAX_ROW + part + 1],
                                 m.maxT[part * H:(part + 1) * H]).then_inc(max_packed, 16)
                if isinstance(b, int) and b < 2:
                    pass
                else:
                    store_x(ph, b - 2)
                if front:
                    store_q_k(*front)
                    if not last:
                        reached(sp, load_seen, scores_full, ph.scores(b) + ph.units)
                    fetch_q_k(*front, target_parity(ph, par, last))
                load_residual(ph, b)
                if last:
                    reached(sp, load_seen, front_full, ph.next.at(0, ph.next.last_T))
                    load_inputs(ph.next, 1)

            def step_l1(ph, b, par, first, last):
                front = front_target(ph, b, last)
                if isinstance(b, int) and b < 2:
                    store_x(ph.prev, B - 2 + b)
                else:
                    store_x(ph, b - 2)
                if front:
                    store_q_k(*front)
                    reached(sp, load_seen, scores_full, ph.scores(b))
                    fetch_q_k(*front, target_parity(ph, par, last))
                    reached(sp, load_seen, front_full, front[0].at(front[1], front[0].last_T))
                    if last:
                        load_inputs(ph.next, 1)
                    elif isinstance(b, int) and b == B - 2:
                        if ph.next:
                            load_inputs(ph.next, 0)
                    else:
                        load_inputs(ph, b + 2)
                load_residual(ph, b)

            for ph in phases:
                over_batch(sp, lambda *at: (step_l0 if ph.l0 else step_l1)(ph, *at))
            store_x(ph, B - 2)
            ffn.load(sp, load_seen, 0, x_stored, 2 * B)
            store_x(ph, B - 1)
            ffn.loads(sp, load_seen, x_stored, 2 * B)
            reached(sp, load_seen, x_stored, 16 * 3 * B)

        @block.tensor
        def _(pe):
            def mm(out, lhsT, rhs, k=0, n=1):
                return nc.tensor.matmul(out, lhsT, rhs, start=(k == 0), stop=(k == n - 1))

            def front_bank(ph, b, job):
                after(pe, front_free, ph.at(b, job) - 1)

            def transposes(ph, b, job):
                src = m.xin if job == "x" else m.cin
                front_bank(ph, b, job)
                pe.wait_ge(*((x_in, ph.g(b) * 16 + 16) if job == "x" else (c_in, ph.c(b) * 16 + 16)))
                for t in range(T):
                    for k in range(KT):
                        last = nc.tensor.transpose(m.ps_front[:, k * S + t * P:k * S + (t + 1) * P],
                                                   src[:, t, k * P:(k + 1) * P], m.ident_f[:])
                last.then_inc(front_full, 1)

            def transpose_inputs(ph, b):
                transposes(ph, b, "x")
                if not ph.own_kv:
                    transposes(ph, b, "c")

            def project_qk(ph, b, job):
                front_bank(ph, b, job)
                srcT = m.xT if job == "q" or ph.own_kv else m.cT
                for mt in range(KT):
                    for k in range(KT):
                        last = mm(m.ps_front[:, mt * S:(mt + 1) * S],
                                  ph.w[job][:, k, mt * P:(mt + 1) * P], srcT[:, k, :], k, KT)
                last.then_inc(front_full, 1)

            def project_v(ph, b):
                front_bank(ph, b, "v")
                srcT = m.xT if ph.own_kv else m.cT
                for t in range(T):
                    for k in range(KT):
                        last = mm(m.ps_front[:, t * D:(t + 1) * D], srcT[:, k, t * P:(t + 1) * P],
                                  ph.w["v"][:, k, :], k, KT)
                last.then_inc(front_full, 1)

            def scores(ph, b, par, u):
                if u == 0:
                    pe.wait_ge(q_packed, ph.g(b) * PACK + PACK)
                    pe.wait_ge(k_packed, ph.g(b) * PACK + PACK)
                    if ph.l0:
                        pe.wait_ge(max_packed, b * MAXROWS + MAXROWS)
                whole = isinstance(b, int) and b == 0 and u < 2
                after(pe, exp_done, ph.scores(b) + (0 if whole else u - 1))
                rows = ROWS + NPART if ph.l0 else ROWS
                for i in range(ph.heads):
                    h = u * ph.heads + i
                    bank = (u % 2) * ph.heads + i
                    for kt in range(T):
                        last = mm(m.ps_scores[:, bank, kt * S:(kt + 1) * S],
                                  m.kp[par][0:rows, h, kt * P:(kt + 1) * P], m.qp[par][0:rows, h, :])
                last.then_inc(scores_full, 1)

            def max_scores(b, par, u):
                if u == 0:
                    pe.wait_ge(q_packed, b * PACK + PACK)
                    pe.wait_ge(k_packed, b * PACK + PACK)
                    after(pe, maxT_out, b)
                after(pe, max_done, b * NM + u - 1)
                t, h0 = u // (H // 2), 2 * (u % (H // 2))
                for i in range(2):
                    last = mm(m.ps_scores[:, 2 + u % 2, i * S:(i + 1) * S],
                              m.qp[par][0:ROWS, h0 + i, t * P:(t + 1) * P], m.kp[par][0:ROWS, h0 + i, :])
                last.then_inc(max_full, 1)

            def transpose_max(b):
                pe.wait_ge(max_parts, b + 1)
                out = m.ps_scores[:, 2, 0:P].bitcast(BF16)
                for t in range(T):
                    last = nc.tensor.transpose(out[:, t * P:(t + 1) * P],
                                               m.mparts[:, t].rearrange("p c h -> p (c h)"), m.ident_b[:])
                last.then_inc(maxT_full, 1)

            def attend(ph, b, par, quad):
                if ph.l0:
                    pe.wait_ge(exp_done, ph.scores(b) + 4 * (quad + 1))
                else:
                    pe.wait_ge(clip_done, ph.clip(b) + 2 * (quad + 1))
                if quad == 0:
                    pe.wait_ge(front_free, ph.at(b, "v"))
                after(pe, acc_out, ph.g(b) * QUADS + quad - 1)
                for kt in range(T):
                    for j in range(4):
                        last = mm(m.ps_acc[32 * j:32 * j + 32, quad % 2, 0:S],
                                  m.vaug[par][:, kt, 4 * quad + j, :], m.probs[quad % 2][:, j, kt, :], kt, T)
                last.then_inc(acc_full, 1)

            def tail_bank(ph, b, i):
                after(pe, tail_free, ph.g(b) * NTAIL + i)

            def context_rows(ph, b, half):
                tail_bank(ph, b, half)
                pe.wait_ge(acc_out, ph.g(b) * QUADS + 2 * half + 2)
                for t in range(T):
                    for q2 in range(2):
                        at = (t * 2 + q2) * P
                        last = nc.tensor.transpose(m.ps_tail[:, at:at + P],
                                                   m.acc[:, 2 * half + q2, t * P:(t + 1) * P], m.ident_f[:])
                last.then_inc(tail_full, 1)

            def context_back(ph, b):
                tail_bank(ph, b, 2)
                pe.wait_ge(norm_done, ph.g(b) * 2 + 2)
                for t in range(T):
                    for k in range(KT):
                        last = nc.tensor.transpose(m.ps_tail[:, k * S + t * P:k * S + (t + 1) * P],
                                                   m.ctx[:, t, k * P:(k + 1) * P], m.ident_f[:])
                last.then_inc(tail_full, 1)

            def project_out(ph, b):
                tail_bank(ph, b, 3)
                for t in range(T):
                    for k in range(KT):
                        last = mm(m.ps_tail[:, t * D:(t + 1) * D], m.ctxT[:, k, t * P:(t + 1) * P],
                                  ph.w["o"][:, k, :], k, KT)
                last.then_inc(tail_full, 1)

            pe.wait_ge(ident_ready, 1)
            transpose_inputs(L0, 0)
            pe.wait_ge(now_in, 16 * len(now))
            for b in range(2):
                if b:
                    transpose_inputs(L0, b)
                project_qk(L0, b, "q")
                project_qk(L0, b, "k")
                if b == 0:
                    project_v(L0, b)
            pe.wait_ge(later_in, 16 * len(later))
            pe.wait_ge(ones_ready, 1)
            for u in range(NM):
                max_scores(0, 0, u)

            def step_l0(ph, b, par, first, last):
                front, old = front_target(ph, b, last), tail_target(ph, b, first)

                def maxima(*units):
                    for u in units if not last else ():
                        max_scores(b + 1, 1 - par, u)

                def heads(*units):
                    for u in units:
                        scores(ph, b, par, u)

                if old:
                    context_rows(*old, 0)
                    attend(*old, 1 - par, QUADS - 1)
                if not last:
                    project_v(ph, b + 1)
                transpose_max(b)
                if old:
                    context_rows(*old, 1)
                if front:
                    transposes(*front, "x")
                maxima(0, 1)
                if front and not front[0].own_kv:
                    transposes(*front, "c")
                maxima(2)
                if front:
                    project_qk(*front, "q")
                maxima(3)
                heads(0, 1)
                maxima(4)
                if old:
                    context_back(*old)
                heads(2, 3)
                if front:
                    project_qk(*front, "k")
                heads(4)
                attend(ph, b, par, 0)
                maxima(5)
                heads(5, 6)
                maxima(6)
                heads(7)
                maxima(7)
                heads(8, 9)
                attend(ph, b, par, 1)
                maxima(8)
                heads(10)
                maxima(9)
                heads(11)
                maxima(10)
                heads(12)
                attend(ph, b, par, 2)
                maxima(11)
                heads(13)
                maxima(12)
                heads(14)
                maxima(13)
                heads(15)
                if old:
                    project_out(*old)
                maxima(14, 15)
                if last:
                    project_v(*front)

            def step_l1(ph, b, par, first, last):
                front, old = front_target(ph, b, last), tail_target(ph, b, first)
                scores(ph, b, par, 0)
                context_rows(*old, 0)
                if front:
                    transposes(*front, "x")
                attend(*old, 1 - par, QUADS - 1)
                scores(ph, b, par, 1)
                if front and not front[0].own_kv:
                    transposes(*front, "c")
                if front:
                    project_qk(*front, "q")
                context_rows(*old, 1)
                scores(ph, b, par, 2)
                if front:
                    project_qk(*front, "k")
                attend(ph, b, par, 0)
                context_back(*old)
                scores(ph, b, par, 3)
                if front:
                    project_v(*front)
                scores(ph, b, par, 4)
                attend(ph, b, par, 1)
                scores(ph, b, par, 5)
                project_out(*old)
                scores(ph, b, par, 6)
                attend(ph, b, par, 2)
                scores(ph, b, par, 7)

            for ph in phases:
                over_batch(pe, lambda *at: (step_l0 if ph.l0 else step_l1)(ph, *at))
            ffn.transposes(pe, 0, exp_done, ph.scores(B))
            context_rows(ph, B - 1, 0)
            attend(ph, B - 1, (B - 1) % 2, QUADS - 1)
            context_rows(ph, B - 1, 1)
            context_back(ph, B - 1)
            project_out(ph, B - 1)
            ffn.products(pe, acc_out, ph.g(B) * QUADS)

        @block.scalar
        def _(act):
            def evac_T(ph, b, job):
                act.wait_ge(front_full, ph.at(b, job))
                dst = m.xT if job == "x" else m.cT
                nc.scalar.copy(dst[:].rearrange("p k n -> p (k n)"), m.ps_front[:]).then_inc(front_free, 1)

            def high_part(ph, b, job):
                parts, stored = (m.qs, q_stored) if job == "q" else (m.ks, k_stored)
                act.wait_ge(front_full, ph.at(b, job))
                after(act, stored, ph.g(b) * 16)
                if ph.l0:
                    for mt in range(KT):
                        last = nc.scalar.activation(parts[:, 0, mt, :], m.ps_front[:, mt * S:(mt + 1) * S],
                                                    ACT.Identity, bias=ph.w["b" + job][:, mt:mt + 1])
                else:
                    last = nc.scalar.copy(parts[:, 0].rearrange("p m n -> p (m n)"), m.ps_front[:])
                last.then_inc(part_h, 1)

            def evac_v(ph, b, par):
                act.wait_ge(front_full, ph.at(b, "v"))
                nc.scalar.copy(m.vaug[par][:, :, :, 0:DH],
                               m.ps_front[:].rearrange("p (t h d) -> p t h d", t=T, h=H)).then_inc(front_free, 1)

            def exp(ph, b, u):
                act.wait_ge(scores_full, ph.scores(b) + u + 1)
                quad, at = u * ph.heads // 4, u * ph.heads % 4
                after(act, acc_full, ph.g(b) * QUADS + quad - 1)
                bank = (u % 2) * ph.heads
                out = m.probs[quad % 2][:, at:at + ph.heads].rearrange("p h t n -> p h (t n)")
                nc.scalar.activation(out, m.ps_scores[:, bank:bank + ph.heads, :], ACT.Exp,
                                     scale=SCALE).then_inc(exp_done, 1)

            def evac_acc(ph, b, quad):
                act.wait_ge(acc_full, ph.g(b) * QUADS + quad + 1)
                after(act, tail_full, ph.g(b) * NTAIL - NTAIL + 1 + quad // 2)
                nc.scalar.copy(m.acc[:, quad, :], m.ps_acc[:, quad % 2, 0:S]).then_inc(acc_out, 1)

            def evac_ctxT(ph, b):
                act.wait_ge(tail_full, ph.g(b) * NTAIL + 3)
                nc.scalar.copy(m.ctxT[:].rearrange("p k n -> p (k n)"), m.ps_tail[:]).then_inc(tail_free, 1)

            def evac_maxT(b):
                act.wait_ge(maxT_full, b + 1)
                after(act, max_packed, b * MAXROWS)
                nc.scalar.copy(m.maxT[:], m.ps_scores[:, 2, 0:P].bitcast(BF16)[0:NPART * H, :]
                               ).then_inc(maxT_out, 1)

            def evac_inputs(ph, b):
                evac_T(ph, b, "x")
                if not ph.own_kv:
                    evac_T(ph, b, "c")

            for b in range(2):
                evac_inputs(L0, b)
                if b == 0:
                    act.wait_ge(now_in, 16 * len(now))
                high_part(L0, b, "q")
                high_part(L0, b, "k")

            def step_l0(ph, b, par, first, last):
                front, old = front_target(ph, b, last), tail_target(ph, b, first)
                if old:
                    evac_acc(*old, QUADS - 1)
                evac_maxT(b)
                if front:
                    evac_inputs(*front)
                    high_part(*front, "q")
                exp(ph, b, 0)
                exp(ph, b, 1)
                if old:
                    evac_ctxT(*old)
                exp(ph, b, 2)
                exp(ph, b, 3)
                if front:
                    high_part(*front, "k")
                exp(ph, b, 4)
                evac_acc(ph, b, 0)
                for u in range(5, 10):
                    exp(ph, b, u)
                evac_acc(ph, b, 1)
                for u in range(10, 13):
                    exp(ph, b, u)
                evac_acc(ph, b, 2)
                for u in range(13, H):
                    exp(ph, b, u)
                if last:
                    evac_v(*front, 0)

            def step_l1(ph, b, par, first, last):
                front, old = front_target(ph, b, last), tail_target(ph, b, first)
                exp(ph, b, 0)
                if front:
                    evac_T(*front, "x")
                evac_acc(*old, QUADS - 1)
                exp(ph, b, 1)
                if front and not front[0].own_kv:
                    evac_T(*front, "c")
                if front:
                    high_part(*front, "q")
                exp(ph, b, 2)
                if front:
                    high_part(*front, "k")
                evac_acc(ph, b, 0)
                evac_ctxT(*old)
                exp(ph, b, 3)
                if front:
                    evac_v(*front, target_parity(ph, par, last))
                exp(ph, b, 4)
                evac_acc(ph, b, 1)
                exp(ph, b, 5)
                exp(ph, b, 6)
                evac_acc(ph, b, 2)
                exp(ph, b, 7)

            for ph in phases:
                over_batch(act, lambda *at: (step_l0 if ph.l0 else step_l1)(ph, *at))
            ffn.evac_x(act, 0)
            evac_acc(ph, B - 1, QUADS - 1)
            evac_ctxT(ph, B - 1)
            act.wait_ge(later_in, 16 * len(later))
            ffn.gelu(act)

        @block.vector
        def _(dve):
            norm = Chain(dve, dve_norm)
            tail = Chain(dve, dve_tail)
            maxc = Chain(dve, dve_max)

            def lower_parts(ph, b, job):
                parts, stored, i = (m.qs, q_stored, 0) if job == "q" else (m.ks, k_stored, 1)
                dve.wait_ge(part_h, ph.g(b) * 2 + i + 1)
                if i == 0:
                    after(dve, part_l, ph.g(b) * 2)
                after(dve, stored, ph.g(b) * 16)
                if ph.l0:
                    for mt in range(KT):
                        last = nc.vector.scalar_tensor_tensor(
                            m.rest[i][:, mt, :], m.ps_front[:, mt * S:(mt + 1) * S],
                            ph.w["b" + job][:, mt:mt + 1], parts[:, 0, mt, :], ALU.add, ALU.subtract)
                else:
                    last = nc.vector.tensor_tensor(m.rest[i][:].rearrange("p m n -> p (m n)"), m.ps_front[:],
                                                   parts[:, 0].rearrange("p m n -> p (m n)"), ALU.subtract)
                last.then_inc(part_r, 1)
                dve.wait_ge(part_r, ph.g(b) * 2 + i + 1)
                dve.sem_inc(front_free, 1)
                nc.vector.tensor_copy(parts[:, 1], m.rest[i][:]).then_inc(part_m, 1)
                if not ph.l0:
                    dve.wait_ge(part_m, ph.g(b) * 2 + i + 1)
                    nc.vector.tensor_tensor(parts[:, 2], m.rest[i][:], parts[:, 1],
                                            ALU.subtract).then_inc(part_l, 1)

            def evac_v(ph, b, par):
                dve.wait_ge(front_full, ph.at(b, "v"))
                nc.vector.tensor_tensor(
                    m.vaug[par][:, :, :, 0:DH], m.ps_front[:].rearrange("p (t h d) -> p t h d", t=T, h=H),
                    ph.w["bv"][:].rearrange("p t (h d) -> p t h d", h=H), ALU.add).then_inc(front_free, 1)

            def row_max(b, u):
                dve.wait_ge(max_full, b * NM + u + 1)
                if u == 0:
                    after(dve, max_parts, b)
                t, h0 = u // (H // 2), 2 * (u % (H // 2))
                nc.vector.reduce_max(m.rmax[:, t, h0:h0 + 2],
                                     m.ps_scores[:, 2 + u % 2, :].rearrange("p (h n) -> p h n", h=2),
                                     AX_X).then_inc(max_done, 1)

            def split_max(b):
                maxc.start(b * 3)
                dve.wait_ge(max_done, b * NM + NM)
                after(dve, maxT_full, b)
                hp, mp, lp = (m.mparts[:, :, c, :] for c in range(NPART))
                maxc.link(nc.vector.tensor_scalar(hp, m.rmax[:], -1.0, None, ALU.mult))
                maxc.link(nc.vector.scalar_tensor_tensor(m.rrest[:], m.rmax[:], -1.0, hp, ALU.mult, ALU.subtract))
                maxc.link(nc.vector.tensor_copy(mp, m.rrest[:]))
                nc.vector.tensor_tensor(lp, m.rrest[:], mp, ALU.subtract).then_inc(max_parts, 1)

            def clip(ph, b, u):
                dve.wait_ge(exp_done, ph.scores(b) + u + 1)
                quad, at = u // 2, 2 * (u % 2)
                p = m.probs[quad % 2][:, at:at + 2].rearrange("p h t n -> p (h t n)")
                nc.vector.tensor_scalar(p, p, CLIP_LO, CLIP_HI, ALU.max, ALU.min).then_inc(clip_done, 1)

            def normalise(ph, b, half):
                norm.start(ph.norm(b) + half * ph.norm_steps)
                dve.wait_ge(tail_full, ph.g(b) * NTAIL + half + 1)
                if half == 0:
                    after(dve, tail_full, ph.g(b) * NTAIL - 1)
                rowsT = m.ps_tail[:].rearrange("p (t h c) -> p t h c", t=T, c=32)
                den = rowsT[:, :, :, DH]
                shape = (P, T, H // 2)
                if ph.masked:
                    keep = m.maskf[:, bass.ds(b, 1), :].rearrange("p a t -> p (a t)")
                    keep = keep.rearrange("p (t o) -> p t o", o=1).to_broadcast(shape)
                    norm.link(nc.vector.tensor_tensor(m.den[:], den, keep, ALU.mult))
                    norm.link(nc.vector.scalar_tensor_tensor(m.den2[:], m.den[:], 0.0, m.den[:],
                                                             ALU.is_le, ALU.add))
                    norm.link(nc.vector.reciprocal(m.rden[:], m.den2[:]))
                    norm.link(nc.vector.tensor_tensor(m.rden2[:], m.rden[:], keep, ALU.mult))
                    rden = m.rden2
                else:
                    norm.link(nc.vector.tensor_copy(m.den[:], den))
                    norm.link(nc.vector.reciprocal(m.rden[:], m.den[:]))
                    rden = m.rden
                out = m.ctx[:, :, half * P:(half + 1) * P].rearrange("p t (h d) -> p t h d", d=DH)
                nc.vector.tensor_tensor(
                    out, rowsT[:, :, :, 0:DH],
                    rden[:].rearrange("p t (h o) -> p t h o", o=1).to_broadcast((P, T, H // 2, DH)),
                    ALU.mult).then_inc(norm_done, 1)
                dve.wait_ge(norm_done, ph.g(b) * 2 + half + 1)
                dve.sem_inc(tail_free, 1)

            def add_and_stats(ph, b):
                tail.start(ph.g(b) * 2)
                dve.wait_ge(tail_full, ph.g(b) * NTAIL + 4)
                if ph.l0:
                    dve.wait_ge(resid_ready, b + 1)
                else:
                    dve.wait_ge(r_in, ph.g(b) * 16 + 16)
                after(dve, xn_done, ph.g(b))
                nc.vector.tensor_tensor(m.y[:].rearrange("p t d -> p (t d)"), m.ps_tail[:],
                                        m.rin[:].rearrange("p t d -> p (t d)"), ALU.add).then_inc(y_done, 1)
                dve.wait_ge(y_done, ph.g(b) + 1)
                dve.sem_inc(tail_free, 1)
                nc.vector.bn_stats(m.stats[:, 0, :], m.y[:, 0, :])
                tail.link(nc.vector.bn_stats(m.stats[:, 1, :], m.y[:, 1, :]))
                dve.sem_inc(stats_seen, 1)
                nc.vector.bn_aggr(m.mv[:, 0, :], m.stats[:, 0, :])
                tail.link(nc.vector.bn_aggr(m.mv[:, 1, :], m.stats[:, 1, :]))
                dve.sem_inc(var_done, 1)

            def scale_rows(ph, b):
                dve.wait_ge(rstd_done, ph.g(b) + 1)
                after(dve, xo_done, ph.g(b))
                for t in range(T):
                    last = nc.vector.tensor_scalar(m.xn[:, t, :], m.y[:, t, :], m.mv[:, t, 0:1],
                                                   m.rstd[:, t:t + 1], ALU.subtract, ALU.mult)
                last.then_inc(xn_done, 1)

            nc.vector.memset(m.neg_half[:], -0.5)
            for eps, tile in m.eps.items():
                nc.vector.memset(tile[:], eps)
            nc.vector.memset(m.mparts[:], 0.0)
            for par in range(2):
                last = nc.vector.memset(m.vaug[par][:, :, :, DH:], 1.0)
            last.then_inc(consts_ready, 1)
            dve.wait_ge(consts_ready, 1)
            dve.wait_ge(mask_in, 16)
            nc.vector.tensor_copy(m.maskf[:], m.mask_u8[:]).then_inc(mask_ready, 1)
            dve.wait_ge(mask_ready, 1)
            dve.wait_ge(now_in, 16 * len(now))
            for b in range(2):
                lower_parts(L0, b, "q")
                lower_parts(L0, b, "k")
                if b == 0:
                    evac_v(L0, b, b)
            for u in range(NM):
                row_max(0, u)
            split_max(0)

            def step_l0(ph, b, par, first, last):
                front, old = front_target(ph, b, last), tail_target(ph, b, first)

                def maxima(start, end):
                    for u in range(start, end) if not last else ():
                        row_max(b + 1, u)

                if old:
                    normalise(*old, 0)
                if not last:
                    evac_v(ph, b + 1, 1 - par)
                if old:
                    normalise(*old, 1)
                maxima(0, 3)
                if front:
                    lower_parts(*front, "q")
                maxima(3, 5)
                if front:
                    lower_parts(*front, "k")
                maxima(5, 14)
                if old:
                    add_and_stats(*old)
                maxima(14, NM)
                if not last:
                    split_max(b + 1)
                if old:
                    scale_rows(*old)

            def step_l1(ph, b, par, first, last):
                front, old = front_target(ph, b, last), tail_target(ph, b, first)
                clip(ph, b, 0)
                normalise(*old, 0)
                clip(ph, b, 1)
                if front:
                    lower_parts(*front, "q")
                normalise(*old, 1)
                clip(ph, b, 2)
                if front:
                    lower_parts(*front, "k")
                clip(ph, b, 3)
                clip(ph, b, 4)
                clip(ph, b, 5)
                add_and_stats(*old)
                clip(ph, b, 6)
                scale_rows(*old)
                clip(ph, b, 7)

            for ph in phases:
                over_batch(dve, lambda *at: (step_l0 if ph.l0 else step_l1)(ph, *at))
            normalise(ph, B - 1, 0)
            normalise(ph, B - 1, 1)
            add_and_stats(ph, B - 1)
            scale_rows(ph, B - 1)
            ffn.rows(dve, stats_seen)

        @block.gpsimd
        def _(pool):
            tail = Chain(pool, pool_tail)

            def low_part(ph, b, job):
                parts, i = (m.qs, 0) if job == "q" else (m.ks, 1)
                pool.wait_ge(part_m, ph.g(b) * 2 + i + 1)
                nc.gpsimd.tensor_tensor(parts[:, 2], m.rest[i][:], parts[:, 1], ALU.subtract).then_inc(part_l, 1)

            def rstd(ph, b):
                tail.start(ph.g(b) * 2)
                pool.wait_ge(var_done, ph.g(b) + 1)
                tail.link(nc.gpsimd.tensor_tensor(m.vare[:], m.mv[:, :, 1], m.eps[ph.eps][:, 0:T], ALU.add))
                nc.gpsimd.tensor_tensor(m.rstd[:], m.vare[:], m.neg_half[:, 0:T], ALU.pow).then_inc(rstd_done, 1)

            def affine(ph, b):
                tail.start(ph.g(b) * 2 + 1)
                pool.wait_ge(xn_done, ph.g(b) + 1)
                tail.link(nc.gpsimd.tensor_tensor(m.xg[:], m.xn[:], ph.w["gamma"][:], ALU.mult))
                after(pool, x_stored, ph.g(b) * 16)
                nc.gpsimd.tensor_tensor(m.xo[:], m.xg[:], ph.w["beta"][:], ALU.add).then_inc(xo_done, 1)

            def residual(ph, b):
                pool.wait_ge(r_in, ph.g(b) * 16 + 16)
                nc.gpsimd.tensor_tensor(m.rin[:], m.rin[:], ph.w["bo"][:], ALU.add).then_inc(resid_ready, 1)

            nc.gpsimd.memset(m.ident_f[:], 0.0)
            nc.gpsimd.memset(m.ident_b[:], 0.0).then_inc(ident_filled, 1)
            pool.wait_ge(ident_filled, 1)
            for ident in (m.ident_f, m.ident_b):
                last = nc.gpsimd.affine_select(out=ident[:], in_=ident[:], compare_op=ALU.not_equal, fill=1.0,
                                               base=0, pattern=[[-1, P]], channel_multiplier=1)
            last.then_inc(ident_ready, 1)
            pool.wait_ge(ident_ready, 1)
            for par in range(2):
                last = nc.gpsimd.memset(m.kp[par][MAX_ROW:MAX_ROW + NPART], 1.0)
            last.then_inc(ones_ready, 1)
            pool.wait_ge(ones_ready, 1)
            pool.wait_ge(consts_ready, 1)
            for b in range(2):
                low_part(L0, b, "q")
                low_part(L0, b, "k")
            pool.wait_ge(later_in, 16 * len(later))

            def step(ph, b, par, first, last):
                front, old = front_target(ph, b, last), tail_target(ph, b, first)
                if front and front[0].l0:
                    low_part(*front, "q")
                    low_part(*front, "k")
                if old:
                    rstd(*old)
                    affine(*old)
                if ph.l0:
                    residual(ph, b)

            for ph in phases:
                over_batch(pool, lambda *at: step(ph, *at))
            ffn.residual(pool, 0)
            rstd(ph, B - 1)
            affine(ph, B - 1)
            ffn.norm(pool)


class Ffn:

    PAIR = 2
    NT = PAIR * T
    FT = FF // P
    NSTEP = B // PAIR

    def __init__(self, nc, m, x_src, out, w):
        self.nc, self.m, self.x_src, self.out, self.w = nc, m, x_src, out, w

    def semaphores(self, sem):
        self.x_in = sem("ffn_x_in")
        self.xT_full = sem("ffn_xT_full")
        self.xT_out = sem("ffn_xT_out")
        self.up_full = sem("ffn_up_full")
        self.gelu_done = sem("ffn_gelu_done")
        self.down_full = sem("ffn_down_full")
        self.y_done = sem("ffn_y_done")
        self.resid_ready = sem("ffn_resid_ready")
        self.stats_done = sem("ffn_stats_done")
        self.var_done = sem("ffn_var_done")
        self.vare_done = sem("ffn_vare_done")
        self.rstd_done = sem("ffn_rstd_done")
        self.xn_done = sem("ffn_xn_done")
        self.xg_done = sem("ffn_xg_done")
        self.xo_done = sem("ffn_xo_done")
        self.stored = sem("ffn_stored")

    def steps(self, engine, step):
        step(0, True, False)
        with engine.Fori(1, self.NSTEP - 1) as i:
            step(i, False, False)
        step(self.NSTEP - 1, False, True)

    def tok(self, dram, i):
        return dram[bass.ds(i * self.PAIR, self.PAIR)].rearrange("a (t p) d -> p (a t) d", p=P)

    def load(self, sp, seen, i, x_stored, before):
        reached(sp, seen, x_stored, (before + i * self.PAIR + self.PAIR) * 16)
        sp.dma_start(self.m.f_x[:], self.tok(self.x_src, i)).then_inc(self.x_in, 16)

    def loads(self, sp, seen, x_stored, before):
        def store(i):
            reached(sp, seen, self.xo_done, i + 1)
            sp.dma_start(self.tok(self.out, i), self.m.f_xo[:]).then_inc(self.stored, 16)

        def step(i, first, last):
            if not last:
                reached(sp, seen, self.xT_full, i * self.PAIR + self.PAIR)
                reached(sp, seen, self.resid_ready, i + 1)
                self.load(sp, seen, i + 1, x_stored, before)
            if not first:
                store(i - 1)

        self.steps(sp, step)
        store(self.NSTEP - 1)
        reached(sp, seen, self.stored, 16 * self.NSTEP)

    def transposes(self, pe, i, exp_done=None, all_exps=None):
        nc, m = self.nc, self.m
        if exp_done is not None:
            pe.wait_ge(exp_done, all_exps)
        pe.wait_ge(self.x_in, i * 16 + 16)
        for a in range(self.PAIR):
            for t in range(T):
                for k in range(KT):
                    last = nc.tensor.transpose(m.ps_scores[:, a, k * S + t * P:k * S + (t + 1) * P],
                                               m.f_x[:, a * T + t, k * P:(k + 1) * P], m.ident_f[:])
            last.then_inc(self.xT_full, 1)

    def products(self, pe, acc_out, all_out):
        nc, m, w = self.nc, self.m, self.w
        pe.wait_ge(acc_out, all_out)

        def step(i, first, last):
            pe.wait_ge(self.xT_out, i * self.PAIR + self.PAIR)
            for f in range(self.FT):
                if not (first and f < 2):
                    pe.wait_ge(self.gelu_done, i * self.FT + f - 1)
                for k in range(KT):
                    mm = nc.tensor.matmul(m.ps_scores[:, 2 + f % 2, :], w["w1"][:, k, f * P:(f + 1) * P],
                                          m.f_xT[:, k, :], start=(k == 0), stop=(k == KT - 1))
                mm.then_inc(self.up_full, 1)
            if not last:
                self.transposes(pe, i + 1)
            for t in range(self.NT):
                if not (first and t < 2):
                    pe.wait_ge(self.y_done, i * self.NT + t - 1)
                for f in range(self.FT):
                    if t == 0:
                        pe.wait_ge(self.gelu_done, i * self.FT + f + 1)
                    mm = nc.tensor.matmul(m.ps_acc[:, t % 2, 0:D], m.f_h[:, f, t * P:(t + 1) * P],
                                          w["w2"][:, f, :], start=(f == 0), stop=(f == self.FT - 1))
                mm.then_inc(self.down_full, 1)

        self.steps(pe, step)

    def evac_x(self, act, i):
        nc, m = self.nc, self.m
        for a in range(self.PAIR):
            act.wait_ge(self.xT_full, i * self.PAIR + a + 1)
            nc.scalar.copy(m.f_xT[:, :, a * S:(a + 1) * S],
                           m.ps_scores[:, a, :].rearrange("p (k n) -> p k n", k=KT)).then_inc(self.xT_out, 1)

    def gelu(self, act):
        nc, m, w = self.nc, self.m, self.w

        def step(i, first, last):
            for f in range(self.FT):
                act.wait_ge(self.up_full, i * self.FT + f + 1)
                if not first:
                    act.wait_ge(self.down_full, i * self.NT)
                nc.scalar.activation(m.f_h[:, f, :], m.ps_scores[:, 2 + f % 2, :], ACT.Gelu,
                                     bias=w["b1"][:, f:f + 1]).then_inc(self.gelu_done, 1)
            if not last:
                self.evac_x(act, i + 1)

        self.steps(act, step)

    def rows(self, dve, seen):
        nc, m = self.nc, self.m

        def step(i, first, last):
            dve.wait_ge(self.resid_ready, i + 1)
            if not first:
                dve.wait_ge(self.xn_done, i)
            for t in range(self.NT):
                dve.wait_ge(self.down_full, i * self.NT + t + 1)
                nc.vector.tensor_tensor(m.f_y[:, t, :], m.ps_acc[:, t % 2, 0:D], m.f_r[:, t, :],
                                        ALU.add).then_inc(self.y_done, 1)
                dve.wait_ge(self.y_done, i * self.NT + t + 1)
                nc.vector.bn_stats(m.f_stats[:, t, :], m.f_y[:, t, :]).then_inc(self.stats_done, 1)
                dve.wait_ge(self.stats_done, i * self.NT + t + 1)
                dve.sem_inc(seen, 1)
                nc.vector.bn_aggr(m.f_mv[:, t, :], m.f_stats[:, t, :]).then_inc(self.var_done, 1)
            dve.wait_ge(self.rstd_done, i + 1)
            if not first:
                dve.wait_ge(self.xg_done, i)
            for t in range(self.NT):
                xn = nc.vector.tensor_scalar(m.f_xn[:, t, :], m.f_y[:, t, :], m.f_mv[:, t, 0:1],
                                             m.f_rstd[:, t:t + 1], ALU.subtract, ALU.mult)
            xn.then_inc(self.xn_done, 1)

        self.steps(dve, step)

    def residual(self, pool, i):
        nc, m = self.nc, self.m
        pool.wait_ge(self.x_in, i * 16 + 16)
        for a in range(self.PAIR):
            r = nc.gpsimd.tensor_tensor(m.f_r[:, a * T:(a + 1) * T], m.f_x[:, a * T:(a + 1) * T],
                                        self.w["b2"][:], ALU.add)
        r.then_inc(self.resid_ready, 1)

    def norm(self, pool):
        nc, m, w = self.nc, self.m, self.w

        def step(i, first, last):
            pool.wait_ge(self.var_done, i * self.NT + self.NT)
            nc.gpsimd.tensor_tensor(m.f_vare[:], m.f_mv[:, :, 1], m.eps[1e-5][:], ALU.add).then_inc(self.vare_done, 1)
            pool.wait_ge(self.vare_done, i + 1)
            nc.gpsimd.tensor_tensor(m.f_rstd[:], m.f_vare[:], m.neg_half[:], ALU.pow).then_inc(self.rstd_done, 1)
            if not last:
                self.residual(pool, i + 1)
            pool.wait_ge(self.xn_done, i + 1)
            for a in range(self.PAIR):
                g = nc.gpsimd.tensor_tensor(m.f_xg[:, a * T:(a + 1) * T], m.f_xn[:, a * T:(a + 1) * T],
                                            w["gamma"][:], ALU.mult)
            g.then_inc(self.xg_done, 1)
            pool.wait_ge(self.xg_done, i + 1)
            if not first:
                pool.wait_ge(self.stored, i * 16)
            for a in range(self.PAIR):
                o = nc.gpsimd.tensor_tensor(m.f_xo[:, a * T:(a + 1) * T], m.f_xg[:, a * T:(a + 1) * T],
                                            w["beta"][:], ALU.add)
            o.then_inc(self.xo_done, 1)

        self.steps(pool, step)


class Memory:
    pass


def build(nc, a, out):
    with ExitStack() as ctx:
        def sb(name, shape, dt=F32):
            return ctx.enter_context(nc.sbuf_tensor(name, shape, dt))

        def pair(name, shape, dt):
            return [sb(f"{name}{i}", shape, dt) for i in range(2)]

        m = Memory()
        m.ident_f, m.ident_b = sb("ident_f", [P, P]), sb("ident_b", [P, P], BF16)
        m.mask_u8, m.maskf = sb("mask_u8", [P, B, T], U8), sb("maskf", [P, B, T])
        m.neg_half = sb("neg_half", [P, 2 * T])
        m.eps = {1e-6: sb("eps_l0", [P, 2 * T]), 1e-5: sb("eps_l1", [P, 2 * T])}
        m.xin, m.cin, m.rin = sb("xin", [P, T, D]), sb("cin", [P, T, D]), sb("rin", [P, T, D])
        m.xT, m.cT = sb("xT", [P, KT, S]), sb("cT", [P, KT, S])
        m.qs, m.ks = sb("q_parts", [P, NPART, KT, S], BF16), sb("k_parts", [P, NPART, KT, S], BF16)
        m.rest = pair("rest", [P, KT, S], F32)
        m.qp, m.kp = pair("q_packed", [P, H, S], BF16), pair("k_packed", [P, H, S], BF16)
        m.vaug = pair("v_ones", [P, T, H, 32], F32)
        m.probs = pair("probs", [P, 4, T, S], F32)
        m.acc = sb("acc", [P, QUADS, S])
        m.rmax, m.rrest = sb("rmax", [P, T, H]), sb("rmax_rest", [P, T, H])
        m.mparts, m.maxT = sb("max_parts", [P, T, P // H, H], BF16), sb("maxT", [NPART * H, S], BF16)
        m.den, m.den2, m.rden, m.rden2 = (sb(n, [P, T, H // 2]) for n in ("den", "den2", "rden", "rden2"))
        m.ctx, m.ctxT = sb("ctx", [P, T, D]), sb("ctxT", [P, KT, S])
        m.y, m.xn, m.xg, m.xo = (sb(n, [P, T, D]) for n in ("y", "xn", "xg", "xo"))
        m.stats, m.mv = sb("stats", [P, T, 6]), sb("mv", [P, T, 2])
        m.vare, m.rstd = sb("vare", [P, T]), sb("rstd", [P, T])
        m.f_x, m.f_r, m.f_y, m.f_xn, m.f_xg, m.f_xo = (
            sb(f"f_{n}", [P, 2 * T, D]) for n in ("x", "r", "y", "xn", "xg", "xo"))
        m.f_xT, m.f_h = sb("f_xT", [P, KT, 2 * S]), sb("f_h", [P, FF // P, 2 * S])
        m.f_stats, m.f_mv = sb("f_stats", [P, 2 * T, 6]), sb("f_mv", [P, 2 * T, 2])
        m.f_vare, m.f_rstd = sb("f_vare", [P, 2 * T]), sb("f_rstd", [P, 2 * T])
        m.ps_scores = ctx.enter_context(nc.psum_tensor("ps_scores", [P, 4, 512], F32))
        m.ps_acc = ctx.enter_context(nc.psum_tensor("ps_acc", [P, 2, 512], F32))
        m.ps_front = ctx.enter_context(nc.psum_tensor("ps_front", [P, 512], F32))
        m.ps_tail = ctx.enter_context(nc.psum_tensor("ps_tail", [P, 512], F32))
        m.q_dram = nc.dram_tensor("q_scratch", (NPART, KT, P, S), BF16, kind="Internal").ap()
        m.k_dram = nc.dram_tensor("k_scratch", (NPART, KT, P, S), BF16, kind="Internal").ap()
        x1 = nc.dram_tensor("x_after_l0", (B, S, D), F32, kind="Internal").ap()
        x2 = nc.dram_tensor("x_after_self", (B, S, D), F32, kind="Internal").ap()
        x3 = nc.dram_tensor("x_after_cross", (B, S, D), F32, kind="Internal").ap()

        def mat(name, dram):
            n = dram.shape[1]
            t = sb(name, [P, dram.shape[0] // P, n])
            return t, (t[:], dram.rearrange("(k p) n -> p k n", p=P))

        def cols(name, vec):
            t = sb(name, [P, vec.shape[0] // P])
            return t, (t[:], vec.rearrange("(m p) -> p m", p=P))

        def row(name, vec):
            t = sb(name, [P, T, D])
            src = vec.rearrange("(o d) -> o d", o=1).to_broadcast((P, D))
            return t, [(t[:, i, :], src) for i in range(T)]

        def weights(prefix, names, kind_cols=(), kind_rows=()):
            w, loads = {}, []
            for key, name in names:
                w[key], load = mat(f"{prefix}_{key}", a[name])
                loads.append(load)
            for key, name in kind_cols:
                w[key], load = cols(f"{prefix}_{key}", a[name])
                loads.append(load)
            for key, name in kind_rows:
                w[key], ls = row(f"{prefix}_{key}", a[name])
                loads += ls
            return w, loads

        w0, l0 = weights("l0", [("q", "L0_xattn_Wq"), ("k", "L0_xattn_Wk"), ("v", "L0_xattn_Wv")],
                         [("bq", "L0_xattn_bq"), ("bk", "L0_xattn_bk")], [("bv", "L0_xattn_bv")])
        w0o, l0o = weights("l0", [("o", "L0_xattn_Wo")], (),
                           [("bo", "L0_xattn_bo"), ("gamma", "L0_xattn_gamma"), ("beta", "L0_xattn_beta")])
        w0.update(w0o)
        ws, ls = weights("sa", [(k, f"L1_xattn_sa_w{k}") for k in "qkvo"], (),
                         [("gamma", "L1_xattn_g1"), ("beta", "L1_xattn_be1")])
        wc, lc = weights("ca", [(k, f"L1_xattn_ca_w{k}") for k in "qkvo"], (),
                         [("gamma", "L1_xattn_g2"), ("beta", "L1_xattn_be2")])
        wf, lf = weights("ff", [("w1", "L1_xattn_w1"), ("w2", "L1_xattn_w2")], [("b1", "L1_xattn_b1")],
                         [("b2", "L1_xattn_b2"), ("gamma", "L1_xattn_g3"), ("beta", "L1_xattn_be3")])
        m.mask_load = m.mask_u8[:], a["mask_BxS_bf1"].rearrange("b (t p) -> p b t", p=P)

        ctx.enter_context(nc.allow_non_contiguous_dma(reason="biases and the mask are laid out once"))
        ctx_in = a["ctx_1024"]
        cross0 = Attention(None, "l0", a["x"], ctx_in, x1, w0, l0=True, eps=1e-6)
        self_attn = Attention(cross0, "sa", x1, None, x2, ws, masked=True)
        cross1 = Attention(self_attn, "ca", x2, ctx_in, x3, wc)
        attention(nc, m, [cross0, self_attn, cross1], l0, l0o + ls + lc + lf, Ffn(nc, m, x3, out, wf))


_INS = ["x", "ctx_1024", "mask_BxS_bf1",
        "L0_xattn_Wv", "L0_xattn_bv", "L0_xattn_Wk", "L0_xattn_bk", "L0_xattn_Wq", "L0_xattn_bq",
        "L0_xattn_Wo", "L0_xattn_bo", "L0_xattn_gamma", "L0_xattn_beta",
        "L1_xattn_sa_wq", "L1_xattn_sa_wk", "L1_xattn_sa_wv", "L1_xattn_sa_wo",
        "L1_xattn_ca_wq", "L1_xattn_ca_wk", "L1_xattn_ca_wv", "L1_xattn_ca_wo",
        "L1_xattn_w1", "L1_xattn_b1", "L1_xattn_w2", "L1_xattn_b2",
        "L1_xattn_g1", "L1_xattn_be1", "L1_xattn_g2", "L1_xattn_be2", "L1_xattn_g3", "L1_xattn_be3"]


def kernel(**inputs):
    import numpy as _np
    import concourse.bacc as _bacc
    from concourse import mybir as _mybir
    from concourse.bass_utils import run_bass_kernel_spmd as _run

    nc = _bacc.Bacc("TRN2", target_bir_lowering=False, num_devices=1)
    arrays, args = {}, {}
    for name in _INS:
        v = _np.ascontiguousarray(inputs[name])
        if v.dtype == _np.bool_:
            v = v.view(_np.uint8)
        arrays[f"in_{name}"] = v
        args[name] = nc.dram_tensor(f"in_{name}", v.shape, _mybir.dt.from_np(v.dtype), kind="ExternalInput").ap()
    out = nc.dram_tensor("out_0", (B, S, D), F32, kind="ExternalOutput").ap()
    build(nc, args, out)
    r = _run(nc, [arrays], core_ids=[0])
    return r.results[0]["out_0"]
```

```python
from contextlib import ExitStack

import numpy as np

import concourse.bass as bass
from concourse import mybir

F32 = mybir.dt.float32
F32R = mybir.dt.float32r
BF16 = mybir.dt.bfloat16
U8 = mybir.dt.uint8
ACT = mybir.ActivationFunctionType
ALU = mybir.AluOpType
AX_X = mybir.AxisListType.X

P = 128
B, S, D = 8, 256, 256
H = 16
DH = D // H
FF = 4 * D
T = S // P
KT = D // P
SCALE = float(DH) ** -0.5
Q_PARTS = (0, 0, 0, 1, 1, 2)
K_PARTS = (0, 1, 2, 0, 1, 0)
ROWS = DH * len(Q_PARTS)
MAX_ROW = ROWS
NPART = 3
QUADS = H // 4
PASSES = ((0, 0), (0, 1), (1, 0))
CLIP_LO, CLIP_HI = float(np.exp(np.float32(-50.0))), float(np.exp(np.float32(50.0)))


def over_batch(engine, step, loop_from=2):
    for b in range(loop_from):
        step(b, b % 2, b == 0, False)
    with engine.Fori(0, (B - 4) // 2) as pair:
        for j in range(2):
            step(pair * 2 + (loop_from + j), (loop_from + j) % 2, False, False)
    for b in range(loop_from + B - 4, B):
        step(b, b % 2, False, b == B - 1)


def after(engine, sem, value):
    if not isinstance(value, int) or value > 0:
        engine.wait_ge(sem, value)


def reached(engine, seen, sem, value):
    if not isinstance(value, int) or value > 0:
        engine.wait_ge(sem, value)
        engine.sem_inc(seen, 1)


class Chain:

    def __init__(self, engine, sem):
        self.engine, self.sem = engine, sem

    def start(self, done):
        self.done = done

    def link(self, ins):
        self.done = self.done + 1
        ins.then_inc(self.sem, 1)
        self.engine.wait_ge(self.sem, self.done)


class Attention:

    def __init__(self, prev, name, q_src, kv_src, out, w, l0=False, masked=False, eps=1e-5):
        self.name, self.q_src, self.kv_src, self.out, self.w = name, q_src, kv_src, out, w
        self.l0 = l0
        self.masked, self.eps = masked, eps
        self.loads, self.loaded = [], None
        self.split = None if l0 else "x" if kv_src is None else "c"
        self.split_keys = "" if l0 else "qkv" if kv_src is None else "kv"
        self.staged = []
        self.w_high = self.w_low = None
        self.own_kv = kv_src is None
        self.prev, self.next = prev, None
        self.jobs = ["x"] + ([] if self.own_kv else ["c"]) + ["q", "k", "v"]
        self.bank = dict(x=0, q=1, k=0, v=1) if self.own_kv else dict(x=0, c=1, q=0, k=1, v=0)
        self.last_T = "x" if self.own_kv else "c"
        self.heads = 1 if l0 else 2
        self.units = H // self.heads
        self.norm_steps = 4 if masked else 2
        self.ahead = 2 if l0 else 1
        if prev is None:
            self.bank0 = 0, 0
            self.g0 = self.front0 = self.scores0 = self.norm0 = self.c0 = self.clip0 = 0
        else:
            prev.next = self
            self.bank0 = tuple(prev.in_bank(B, i) for i in range(2))
            self.g0 = prev.g(B)
            self.front0, self.scores0 = prev.front(B), prev.scores(B)
            self.norm0, self.c0, self.clip0 = prev.norm(B), prev.c(B), prev.clip(B)

    def all_loaded(self, engine):
        engine.wait_ge(self.loaded, 16 * len(self.loads))

    def weights_split(self, engine):
        engine.wait_ge(self.w_low, len(self.staged))

    def g(self, b):
        return b + self.g0

    def front(self, b):
        return b * len(self.jobs) + self.front0

    def halves(self, b):
        return self.g(b) - B + 1

    def in_bank(self, b, bank):
        return b * sum(self.bank[job] == bank for job in self.jobs) + self.bank0[bank]

    def evacuated(self, b, job):
        jobs = [j for j in self.jobs if self.bank[j] == self.bank[job]]
        return self.in_bank(b, self.bank[job]) + jobs.index(job) + 1

    def at(self, b, job):
        return self.front(b) + self.jobs.index(job) + 1

    def scores(self, b):
        return b * self.units + self.scores0

    def clip(self, b):
        return b * (0 if self.l0 else self.units) + self.clip0

    def c(self, b):
        return b * (0 if self.own_kv else 1) + self.c0

    def norm(self, b):
        return b * (2 * self.norm_steps) + self.norm0


def attention(nc, m, phases, first_needed, now, ffn):
    L0, self_attn, cross1 = phases
    NTAIL = 4
    NM = T * H // 2
    PACK = 16 * len(Q_PARTS)

    with ExitStack() as ctx:
        def sem(n):
            return ctx.enter_context(nc.semaphore(n))

        x_in, c_in, r_in = sem("x_in"), sem("c_in"), sem("r_in")
        first_in, now_in = sem("first_in"), sem("now_in")
        for group in phases + [ffn]:
            group.loaded = sem("loaded_" + group.name)
        for ph in (self_attn, cross1):
            ph.w_high, ph.w_low = sem("w_high_" + ph.name), sem("w_low_" + ph.name)
        T_high = sem("T_high")
        mask_in = sem("mask_in")
        ident_filled, ident_ready = sem("ident_filled"), sem("ident_ready")
        consts_ready, ones_ready, mask_ready = sem("consts_ready"), sem("ones_ready"), sem("mask_ready")
        front_full = sem("front_full")
        front_free = sem("front_free_0"), sem("front_free_1")
        tail_full, tail_free = sem("tail_full"), sem("tail_free")
        scores_full, exp_done, clip_done = sem("scores_full"), sem("exp_done"), sem("clip_done")
        max_full, max_done, max_parts = sem("max_full"), sem("max_done"), sem("max_parts")
        maxT_full, maxT_out, max_packed = sem("maxT_full"), sem("maxT_out"), sem("max_packed")
        acc_full, acc_out = sem("acc_full"), sem("acc_out")
        part_h, part_r, part_m, part_l = sem("part_h"), sem("part_r"), sem("part_m"), sem("part_l")
        q_packed, k_packed = sem("q_packed"), sem("k_packed")
        norm_done, resid_ready = sem("norm_done"), sem("resid_ready")
        y_done, var_done, rstd_done = sem("y_done"), sem("var_done"), sem("rstd_done")
        xn_done, xo_done, x_stored = sem("xn_done"), sem("xo_done"), sem("x_stored")
        dve_norm, dve_max, dve_tail, pool_tail = (sem("dve_norm"), sem("dve_max"), sem("dve_tail"),
                                                  sem("pool_tail"))
        stats_seen, load_seen = sem("stats_seen"), sem("load_seen")
        ffn.semaphores(sem)
        block = ctx.enter_context(nc.Block())

        def tok(dram, b):
            return dram[bass.ds(b, 1)].rearrange("a (t p) d -> p (a t) d", p=P)

        def front_target(ph, b, last):
            if last:
                return (ph.next, 0) if ph.next else None
            if ph.l0 and isinstance(b, int) and b + 2 >= B:
                return None
            return ph, b + ph.ahead

        def target_parity(ph, par, last):
            if last:
                return 0
            return par if ph.l0 else 1 - par

        def tail_target(ph, b, first):
            if first:
                return (ph.prev, B - 1) if ph.prev else None
            return ph, b - 1

        @block.sync
        def _(sp):
            def load_inputs(ph, b):
                if ph.prev:
                    after(sp, x_stored, ph.prev.g(b) * 16 + 16)
                    sp.sem_inc(load_seen, 1)
                sp.dma_start(m.xin[:], tok(ph.q_src, b)).then_inc(x_in, 16)
                if not ph.own_kv:
                    sp.dma_start(m.cin[:], tok(ph.kv_src, b)).then_inc(c_in, 16)

            def pack(ph, b, packed, parts, groups, first_part, packed_sem):
                for part, made in enumerate((part_h, part_m, part_l)):
                    reached(sp, load_seen, made, ph.g(b) * 2 + first_part)
                    for g in range(len(groups)):
                        if groups[g] == part:
                            sp.dma_start(packed[g * DH:(g + 1) * DH],
                                         parts[:, part]).then_inc(packed_sem, 16)

            def pack_q_k(ph, b, par):
                pack(ph, b, m.qp[par], m.qs, Q_PARTS, 1, q_packed)
                pack(ph, b, m.kp[par], m.ks, K_PARTS, 2, k_packed)

            def load_residual(ph, b):
                reached(sp, load_seen, y_done, ph.g(b))
                sp.dma_start(m.rin[:], tok(ph.q_src, b)).then_inc(r_in, 16)

            def store_x(ph, b):
                reached(sp, load_seen, xo_done, ph.g(b) + 1)
                sp.dma_start(tok(ph.out, b), m.xo[:]).then_inc(x_stored, 16)

            load_inputs(L0, 0)
            for tile, dram in first_needed:
                sp.dma_start(tile, dram).then_inc(first_in, 16)
            for tile, dram in now:
                sp.dma_start(tile, dram).then_inc(now_in, 16)
            sp.dma_start(*m.mask_load).then_inc(mask_in, 16)
            reached(sp, load_seen, front_full, L0.at(0, "c"))
            load_inputs(L0, 1)
            pack_q_k(L0, 0, 0)
            reached(sp, load_seen, front_full, L0.at(1, "c"))
            load_inputs(L0, 2)
            pack_q_k(L0, 1, 1)

            def load_weights(group):
                for tile, dram in group.loads:
                    sp.dma_start(tile, dram).then_inc(group.loaded, 16)

            def step_l0(ph, b, par, first, last):
                front = front_target(ph, b, last)
                if front:
                    reached(sp, load_seen, front_full, front[0].at(front[1], front[0].last_T))
                if last:
                    load_inputs(ph.next, 1)
                elif isinstance(b, int) and b == B - 3:
                    load_inputs(ph.next, 0)
                elif front:
                    load_inputs(ph, b + 3)
                for at, group in ((0, self_attn), (0, cross1), (B - 2, ffn)):
                    if isinstance(b, int) and b == at:
                        if group is ffn:
                            reached(sp, load_seen, cross1.w_low, len(cross1.staged))
                        load_weights(group)
                if not last:
                    reached(sp, load_seen, maxT_out, b + 2)
                    pack_max(b + 1, 1 - par)
                if front:
                    if not last:
                        reached(sp, load_seen, scores_full, ph.scores(b) + ph.units)
                    pack_q_k(*front, target_parity(ph, par, last))
                load_residual(ph, b)
                if not first:
                    store_x(ph, b - 1)

            def pack_max(b, par):
                sp.dma_start(m.qp[par][MAX_ROW:MAX_ROW + NPART], m.maxT[:]).then_inc(max_packed, 16)

            def step_l1(ph, b, par, first, last):
                front = front_target(ph, b, last)
                if front:
                    reached(sp, load_seen, scores_full, ph.scores(b))
                    reached(sp, load_seen, front_full, front[0].at(front[1], front[0].last_T))
                    if last:
                        load_inputs(ph.next, 1)
                    elif isinstance(b, int) and b == B - 2:
                        if ph.next:
                            load_inputs(ph.next, 0)
                    else:
                        load_inputs(ph, b + 2)
                    pack_q_k(*front, target_parity(ph, par, last))
                load_residual(ph, b)
                store_x(*tail_target(ph, b, first))
                if ph is cross1 and isinstance(b, int) and b == B - 2:
                    ffn.load(sp, load_seen, 0, x_stored, 2 * B)

            reached(sp, load_seen, maxT_out, 1)
            pack_max(0, 0)
            load_weights(L0)
            for ph in phases:
                over_batch(sp, lambda *at: (step_l0 if ph.l0 else step_l1)(ph, *at),
                           loop_from=1 if ph.l0 else 2)
            store_x(ph, B - 1)
            ffn.load_and_store(sp, load_seen, x_stored, 2 * B)
            reached(sp, load_seen, x_stored, 16 * 3 * B)

        @block.tensor
        def _(pe):
            def mm(out, lhsT, rhs, k=0, n=1):
                return nc.tensor.matmul(out, lhsT, rhs, start=(k == 0), stop=(k == n - 1))

            def in_place(ph, b, job):
                pe.wait_ge(front_free[ph.bank[job]], ph.evacuated(b, job))

            def front_bank(ph, b, job):
                after(pe, front_free[ph.bank[job]], ph.evacuated(b, job) - 1)
                return m.ps_front[:, ph.bank[job], :]

            def transposes(ph, b, job):
                src = m.xin if job == "x" else m.cin
                bank = front_bank(ph, b, job)
                pe.wait_ge(*((x_in, ph.g(b) * 16 + 16) if job == "x" else (c_in, ph.c(b) * 16 + 16)))
                for t in range(T):
                    for k in range(KT):
                        last = nc.tensor.transpose(bank[:, k * S + t * P:k * S + (t + 1) * P],
                                                   src[:, t, k * P:(k + 1) * P], m.ident_f[:])
                last.then_inc(front_full, 1)

            def transpose_inputs(ph, b):
                transposes(ph, b, "x")
                if not ph.own_kv:
                    transposes(ph, b, "c")

            def product(out, stationary, moving, split):
                if split:
                    todo = [(stationary(s, k), moving(mv, k)) for k in range(KT) for s, mv in PASSES]
                else:
                    todo = [(stationary(k), moving(k)) for k in range(KT)]
                for n, (lhsT, rhs) in enumerate(todo):
                    last = mm(out, lhsT, rhs, n, len(todo))
                return last

            def project_qk(ph, b, job):
                bank = front_bank(ph, b, job)
                in_place(ph, b, "x" if job == "q" or ph.own_kv else "c")
                srcT = ph.xT if job == "q" or ph.own_kv else ph.cT
                for mt in range(KT):
                    cols = slice(mt * P, (mt + 1) * P)
                    last = product(bank[:, mt * S:(mt + 1) * S], lambda *at: ph.w[job][:, *at, cols],
                                   lambda *at: srcT[:, *at, :], job in ph.split_keys)
                last.then_inc(front_full, 1)

            def project_v(ph, b):
                bank = front_bank(ph, b, "v")
                in_place(ph, b, ph.last_T)
                srcT = ph.xT if ph.own_kv else ph.cT
                for t in range(T):
                    rows = slice(t * P, (t + 1) * P)
                    last = product(bank[:, t * D:(t + 1) * D], lambda *at: srcT[:, *at, rows],
                                   lambda *at: ph.w["v"][:, *at, :], "v" in ph.split_keys)
                last.then_inc(front_full, 1)

            def scores(ph, b, par, u):
                if u == 0:
                    pe.wait_ge(q_packed, ph.g(b) * PACK + PACK)
                    pe.wait_ge(k_packed, ph.g(b) * PACK + PACK)
                    if ph.l0:
                        pe.wait_ge(max_packed, b * 16 + 16)
                whole = isinstance(b, int) and b == 0 and u < 2
                after(pe, exp_done, ph.scores(b) + (0 if whole else u - 1))
                rows = ROWS + NPART if ph.l0 else ROWS
                for i in range(ph.heads):
                    h = u * ph.heads + i
                    bank = (u % 2) * ph.heads + i
                    for kt in range(T):
                        last = mm(m.ps_scores[:, bank, kt * S:(kt + 1) * S],
                                  m.kp[par][0:rows, h, kt * P:(kt + 1) * P], m.qp[par][0:rows, h, :])
                last.then_inc(scores_full, 1)

            def max_scores(b, par, u):
                if u == 0:
                    pe.wait_ge(q_packed, b * PACK + PACK)
                    pe.wait_ge(k_packed, b * PACK + PACK)
                    after(pe, maxT_out, b)
                after(pe, max_done, b * NM + u - 1)
                t, h0 = u // (H // 2), 2 * (u % (H // 2))
                for i in range(2):
                    last = mm(m.ps_scores[:, 2 + u % 2, i * S:(i + 1) * S],
                              m.qp[par][0:ROWS, h0 + i, t * P:(t + 1) * P], m.kp[par][0:ROWS, h0 + i, :])
                last.then_inc(max_full, 1)

            def transpose_max(b):
                pe.wait_ge(max_parts, b + 1)
                out = m.ps_scores[:, 2, 0:P].bitcast(BF16)
                for t in range(T):
                    last = nc.tensor.transpose(out[:, t * P:(t + 1) * P],
                                               m.mparts[:, t].rearrange("p c h -> p (c h)"), m.ident_b[:])
                last.then_inc(maxT_full, 1)

            def attend(ph, b, par, quad):
                if ph.l0:
                    pe.wait_ge(exp_done, ph.scores(b) + 4 * (quad + 1))
                else:
                    pe.wait_ge(clip_done, ph.clip(b) + 2 * (quad + 1))
                if quad == 0:
                    in_place(ph, b, "v")
                after(pe, acc_out, ph.g(b) * QUADS + quad)
                for kt in range(T):
                    for j in range(4):
                        last = mm(m.ps_acc[32 * j:32 * j + 32, (quad % 2) * S:(quad % 2 + 1) * S],
                                  m.vaug[par][:, kt, 4 * quad + j, :], m.probs[quad % 2][:, j, kt, :], kt, T)
                last.then_inc(acc_full, 1)

            def tail_bank(ph, b, i):
                after(pe, tail_free, ph.g(b) * NTAIL + i)

            def context_rows(ph, b, half):
                tail_bank(ph, b, half)
                pe.wait_ge(acc_out, ph.g(b) * QUADS + 2 * half + 2)
                for t in range(T):
                    for q2 in range(2):
                        at = (t * 2 + q2) * P
                        last = nc.tensor.transpose(m.ps_tail[:, at:at + P],
                                                   m.acc[:, 2 * half + q2, t * P:(t + 1) * P], m.ident_f[:])
                last.then_inc(tail_full, 1)

            def context_back(ph, b):
                tail_bank(ph, b, 2)
                pe.wait_ge(norm_done, ph.g(b) * 2 + 2)
                for t in range(T):
                    for k in range(KT):
                        last = nc.tensor.transpose(m.ps_tail[:, k * S + t * P:k * S + (t + 1) * P],
                                                   m.ctx[:, t, k * P:(k + 1) * P], m.ident_f[:])
                last.then_inc(tail_full, 1)

            def project_out(ph, b):
                tail_bank(ph, b, 3)
                for t in range(T):
                    rows = slice(t * P, (t + 1) * P)
                    last = product(m.ps_tail[:, t * D:(t + 1) * D], lambda k: m.ctxT[:, k, rows],
                                   lambda k: ph.w["o"][:, k, :], False)
                last.then_inc(tail_full, 1)

            pe.wait_ge(ident_ready, 1)
            transpose_inputs(L0, 0)
            pe.wait_ge(first_in, 16 * len(first_needed))
            for b in range(2):
                if b:
                    transpose_inputs(L0, b)
                project_qk(L0, b, "q")
                if b == 0:
                    pe.wait_ge(now_in, 16 * len(now))
                project_qk(L0, b, "k")
                if b == 0:
                    project_v(L0, b)
            pe.wait_ge(ones_ready, 1)
            max_scores(0, 0, 0)
            max_scores(0, 0, 1)
            project_v(L0, 1)
            for u in range(2, NM):
                max_scores(0, 0, u)
            transpose_max(0)

            def step_l0(ph, b, par, first, last):
                front, old = front_target(ph, b, last), tail_target(ph, b, first)

                def maxima(*units):
                    for u in units if not last else ():
                        max_scores(b + 1, 1 - par, u)

                def heads(*units):
                    for u in units:
                        scores(ph, b, par, u)

                if last:
                    ph.next.weights_split(pe)
                if not (first or last):
                    project_v(ph, b + 1)
                if old:
                    attend(*old, 1 - par, QUADS - 1)
                    context_rows(*old, 0)
                heads(0, 1, 2)
                if front:
                    transposes(*front, "x")
                heads(3)
                if front and not front[0].own_kv:
                    transposes(*front, "c")
                if old:
                    context_rows(*old, 1)
                if front:
                    project_qk(*front, "q")
                heads(4)
                if old:
                    context_back(*old)
                attend(ph, b, par, 0)
                if front:
                    project_qk(*front, "k")
                heads(5)
                maxima(0, 1)
                heads(6)
                maxima(2)
                heads(7)
                maxima(3)
                heads(8)
                attend(ph, b, par, 1)
                maxima(4, 5)
                for u in range(9, 12):
                    heads(u)
                    maxima(u - 3)
                heads(12)
                maxima(9)
                attend(ph, b, par, 2)
                if last:
                    project_v(*front)
                maxima(10, 11)
                heads(13)
                maxima(12, 13)
                heads(14)
                maxima(14, 15)
                if old:
                    project_out(*old)
                heads(15)
                if not last:
                    transpose_max(b + 1)
                if first:
                    ph.all_loaded(pe)

            def step_l1(ph, b, par, first, last):
                front, old = front_target(ph, b, last), tail_target(ph, b, first)
                if last and ph.next:
                    ph.next.weights_split(pe)
                if front:
                    transposes(*front, "x")
                scores(ph, b, par, 0)
                context_rows(*old, 0)
                scores(ph, b, par, 1)
                attend(*old, 1 - par, QUADS - 1)
                if front and not front[0].own_kv:
                    transposes(*front, "c")
                scores(ph, b, par, 2)
                if front:
                    project_qk(*front, "q")
                attend(ph, b, par, 0)
                context_rows(*old, 1)
                scores(ph, b, par, 3)
                if front:
                    project_qk(*front, "k")
                context_back(*old)
                scores(ph, b, par, 4)
                if front:
                    project_v(*front)
                attend(ph, b, par, 1)
                scores(ph, b, par, 5)
                project_out(*old)
                scores(ph, b, par, 6)
                attend(ph, b, par, 2)
                scores(ph, b, par, 7)

            for ph in phases:
                over_batch(pe, lambda *at: (step_l0 if ph.l0 else step_l1)(ph, *at))
            pe.wait_ge(exp_done, ph.scores(B))
            ffn.transposes(pe, 0)
            ffn.weights_split(pe)
            context_rows(ph, B - 1, 0)
            attend(ph, B - 1, (B - 1) % 2, QUADS - 1)
            ffn.up(pe, 0, 0, True)
            context_rows(ph, B - 1, 1)
            ffn.up(pe, 0, 1, True)
            context_back(ph, B - 1)
            ffn.up(pe, 0, 2, True)
            project_out(ph, B - 1)
            pe.wait_ge(acc_out, ph.g(B) * QUADS)
            ffn.down(pe, 0, 0, True)
            for f in range(3, ffn.FT):
                if f == ffn.FT - 1:
                    ffn.transposes(pe, 1)
                ffn.up(pe, 0, f, True)
                ffn.down(pe, 0, f - ffn.LAG, True)
            ffn.products(pe)

        @block.scalar
        def _(act):
            def evac_T(ph, b, job):
                act.wait_ge(front_full, ph.at(b, job))
                dst = ph.xT if job == "x" else ph.cT
                high = dst[:, 0] if job == ph.split else dst[:]
                nc.scalar.copy(high.rearrange("p k n -> p (k n)"), m.ps_front[:, ph.bank[job]]
                               ).then_inc(T_high if job == ph.split else front_free[ph.bank[job]], 1)

            def high_part(ph, b, job):
                parts, packed = (m.qs, q_packed) if job == "q" else (m.ks, k_packed)
                act.wait_ge(front_full, ph.at(b, job))
                after(act, packed, ph.g(b) * PACK)
                if ph.l0:
                    for mt in range(KT):
                        last = nc.scalar.activation(parts[:, 0, mt, :],
                                                    m.ps_front[:, ph.bank[job], mt * S:(mt + 1) * S],
                                                    ACT.Identity, bias=ph.w["b" + job][:, mt:mt + 1])
                else:
                    last = nc.scalar.copy(parts[:, 0].rearrange("p m n -> p (m n)"), m.ps_front[:, ph.bank[job]])
                last.then_inc(part_h, 1)

            def evac_v(ph, b, par):
                act.wait_ge(front_full, ph.at(b, "v"))
                nc.scalar.copy(m.vaug[par][:, :, :, 0:DH],
                               m.ps_front[:, ph.bank["v"]].rearrange("p (t h d) -> p t h d", t=T, h=H)
                               ).then_inc(front_free[ph.bank["v"]], 1)

            def exp(ph, b, u):
                act.wait_ge(scores_full, ph.scores(b) + u + 1)
                quad, at = u * ph.heads // 4, u * ph.heads % 4
                after(act, acc_full, ph.g(b) * QUADS + quad - 1)
                bank = (u % 2) * ph.heads
                out = m.probs[quad % 2][:, at:at + ph.heads].rearrange("p h t n -> p h (t n)")
                nc.scalar.activation(out, m.ps_scores[:, bank:bank + ph.heads, :], ACT.Exp,
                                     scale=SCALE).then_inc(exp_done, 1)

            def evac_acc(ph, b, quad):
                act.wait_ge(acc_full, ph.g(b) * QUADS + quad + 1)
                after(act, tail_full, ph.g(b) * NTAIL - NTAIL + 1 + quad // 2)
                nc.scalar.copy(m.acc[:, quad, :], m.ps_acc[:, (quad % 2) * S:(quad % 2 + 1) * S]).then_inc(acc_out, 1)

            def evac_ctxT(ph, b):
                act.wait_ge(tail_full, ph.g(b) * NTAIL + 3)
                nc.scalar.copy(m.ctxT[:].rearrange("p k n -> p (k n)"), m.ps_tail[:]).then_inc(tail_free, 1)

            def evac_maxT(b):
                act.wait_ge(maxT_full, b + 1)
                after(act, max_packed, b * 16)
                nc.scalar.copy(m.maxT[:], m.ps_scores[:, 2, 0:P].bitcast(BF16)[0:NPART * H, :]
                               ).then_inc(maxT_out, 1)

            def evac_inputs(ph, b):
                evac_T(ph, b, "x")
                if not ph.own_kv:
                    evac_T(ph, b, "c")

            for b in range(2):
                evac_inputs(L0, b)
                if b == 0:
                    act.wait_ge(first_in, 16 * len(first_needed))
                high_part(L0, b, "q")
                if b == 0:
                    act.wait_ge(now_in, 16 * len(now))
                high_part(L0, b, "k")
            evac_maxT(0)

            def step_l0(ph, b, par, first, last):
                front, old = front_target(ph, b, last), tail_target(ph, b, first)
                if old:
                    evac_acc(*old, QUADS - 1)
                exp(ph, b, 0)
                exp(ph, b, 1)
                exp(ph, b, 2)
                if front:
                    evac_T(*front, "x")
                exp(ph, b, 3)
                if front and not front[0].own_kv:
                    evac_T(*front, "c")
                if front:
                    high_part(*front, "q")
                exp(ph, b, 4)
                if old:
                    evac_ctxT(*old)
                evac_acc(ph, b, 0)
                if front:
                    high_part(*front, "k")
                for u in range(5, 9):
                    exp(ph, b, u)
                evac_acc(ph, b, 1)
                for u in range(9, 13):
                    exp(ph, b, u)
                evac_acc(ph, b, 2)
                if last:
                    evac_v(*front, 0)
                for u in range(13, H):
                    exp(ph, b, u)
                if not last:
                    evac_maxT(b + 1)

            def step_l1(ph, b, par, first, last):
                front, old = front_target(ph, b, last), tail_target(ph, b, first)
                if front:
                    evac_T(*front, "x")
                exp(ph, b, 0)
                exp(ph, b, 1)
                evac_acc(*old, QUADS - 1)
                if front and not front[0].own_kv:
                    evac_T(*front, "c")
                exp(ph, b, 2)
                if front:
                    high_part(*front, "q")
                evac_acc(ph, b, 0)
                exp(ph, b, 3)
                if front:
                    high_part(*front, "k")
                evac_ctxT(*old)
                exp(ph, b, 4)
                if front:
                    evac_v(*front, target_parity(ph, par, last))
                if ph is self_attn and isinstance(b, int):
                    ffn.high_weights(act, ffn.QUARTER_AT.index(b))
                evac_acc(ph, b, 1)
                exp(ph, b, 5)
                exp(ph, b, 6)
                evac_acc(ph, b, 2)
                exp(ph, b, 7)

            for ph in phases:
                over_batch(act, lambda *at: (step_l0 if ph.l0 else step_l1)(ph, *at))
            ffn.evac_x(act, 0)
            evac_acc(ph, B - 1, QUADS - 1)
            ffn.all_loaded(act)
            ffn.gelu(act, 0, 0, True)
            ffn.gelu(act, 0, 1, True)
            evac_ctxT(ph, B - 1)
            for f in range(2, ffn.FT):
                ffn.gelu(act, 0, f, True)
            ffn.gelus(act)

        @block.vector
        def _(dve):
            norm = Chain(dve, dve_norm)
            tail = Chain(dve, dve_tail)
            maxc = Chain(dve, dve_max)

            def lower_parts(ph, b, job):
                parts, packed, i = (m.qs, q_packed, 0) if job == "q" else (m.ks, k_packed, 1)
                dve.wait_ge(part_h, ph.g(b) * 2 + i + 1)
                if i == 0:
                    after(dve, part_l, ph.g(b) * 2)
                after(dve, packed, ph.g(b) * PACK)
                if ph.l0:
                    for mt in range(KT):
                        last = nc.vector.scalar_tensor_tensor(
                            m.rest[i][:, mt, :], m.ps_front[:, ph.bank[job], mt * S:(mt + 1) * S],
                            ph.w["b" + job][:, mt:mt + 1], parts[:, 0, mt, :], ALU.add, ALU.subtract)
                else:
                    last = nc.vector.tensor_tensor(m.rest[i][:].rearrange("p m n -> p (m n)"),
                                                   m.ps_front[:, ph.bank[job]],
                                                   parts[:, 0].rearrange("p m n -> p (m n)"), ALU.subtract)
                last.then_inc(part_r, 1)
                dve.wait_ge(part_r, ph.g(b) * 2 + i + 1)
                dve.sem_inc(front_free[ph.bank[job]], 1)
                nc.vector.tensor_copy(parts[:, 1], m.rest[i][:]).then_inc(part_m, 1)

            def low_T(ph, b, job):
                if job == ph.split:
                    dst = ph.xT if job == "x" else ph.cT
                    dve.wait_ge(T_high, ph.halves(b))
                    nc.vector.tensor_tensor(dst[:, 1].rearrange("p k n -> p (k n)"), m.ps_front[:, ph.bank[job]],
                                            dst[:, 0].rearrange("p k n -> p (k n)").bitcast(F32),
                                            ALU.subtract).then_inc(front_free[ph.bank[job]], 1)

            def evac_v(ph, b, par):
                dve.wait_ge(front_full, ph.at(b, "v"))
                nc.vector.tensor_tensor(
                    m.vaug[par][:, :, :, 0:DH],
                    m.ps_front[:, ph.bank["v"]].rearrange("p (t h d) -> p t h d", t=T, h=H),
                    ph.w["bv"][:].rearrange("p t (h d) -> p t h d", h=H), ALU.add
                ).then_inc(front_free[ph.bank["v"]], 1)

            def row_max(b, u):
                dve.wait_ge(max_full, b * NM + u + 1)
                if u == 0:
                    after(dve, max_parts, b)
                t, h0 = u // (H // 2), 2 * (u % (H // 2))
                nc.vector.reduce_max(m.rmax[:, t, h0:h0 + 2],
                                     m.ps_scores[:, 2 + u % 2, :].rearrange("p (h n) -> p h n", h=2),
                                     AX_X).then_inc(max_done, 1)

            def split_max(b):
                maxc.start(b * 3)
                dve.wait_ge(max_done, b * NM + NM)
                after(dve, maxT_full, b)
                hp, mp, lp = (m.mparts[:, :, c, :] for c in range(NPART))
                maxc.link(nc.vector.tensor_scalar(hp, m.rmax[:], -1.0, None, ALU.mult))
                maxc.link(nc.vector.scalar_tensor_tensor(m.rrest[:], m.rmax[:], -1.0, hp, ALU.mult, ALU.subtract))
                maxc.link(nc.vector.tensor_copy(mp, m.rrest[:]))
                nc.vector.tensor_tensor(lp, m.rrest[:], mp, ALU.subtract).then_inc(max_parts, 1)

            def clip(ph, b, u):
                dve.wait_ge(exp_done, ph.scores(b) + u + 1)
                quad, at = u // 2, 2 * (u % 2)
                p = m.probs[quad % 2][:, at:at + 2].rearrange("p h t n -> p (h t n)")
                nc.vector.tensor_scalar(p, p, CLIP_LO, CLIP_HI, ALU.max, ALU.min).then_inc(clip_done, 1)

            def normalise(ph, b, half):
                norm.start(ph.norm(b) + half * ph.norm_steps)
                dve.wait_ge(tail_full, ph.g(b) * NTAIL + half + 1)
                if half == 0:
                    after(dve, tail_full, ph.g(b) * NTAIL - 1)
                rowsT = m.ps_tail[:].rearrange("p (t h c) -> p t h c", t=T, c=32)
                den = rowsT[:, :, :, DH]
                shape = (P, T, H // 2)
                if ph.masked:
                    keep = m.maskf[:, bass.ds(b, 1), :].rearrange("p a t -> p (a t)")
                    keep = keep.rearrange("p (t o) -> p t o", o=1).to_broadcast(shape)
                    norm.link(nc.vector.tensor_tensor(m.den[:], den, keep, ALU.mult))
                    norm.link(nc.vector.scalar_tensor_tensor(m.den2[:], m.den[:], 0.0, m.den[:],
                                                             ALU.is_le, ALU.add))
                    norm.link(nc.vector.reciprocal(m.rden[:], m.den2[:]))
                    norm.link(nc.vector.tensor_tensor(m.rden2[:], m.rden[:], keep, ALU.mult))
                    rden = m.rden2
                else:
                    norm.link(nc.vector.tensor_copy(m.den[:], den))
                    norm.link(nc.vector.reciprocal(m.rden[:], m.den[:]))
                    rden = m.rden
                out = m.ctx[:, :, half * P:(half + 1) * P].rearrange("p t (h d) -> p t h d", d=DH)
                nc.vector.tensor_tensor(
                    out, rowsT[:, :, :, 0:DH],
                    rden[:].rearrange("p t (h o) -> p t h o", o=1).to_broadcast((P, T, H // 2, DH)),
                    ALU.mult).then_inc(norm_done, 1)
                dve.wait_ge(norm_done, ph.g(b) * 2 + half + 1)
                dve.sem_inc(tail_free, 1)

            def add_residual(ph, b):
                dve.wait_ge(tail_full, ph.g(b) * NTAIL + 4)
                if ph.l0:
                    dve.wait_ge(resid_ready, b + 1)
                else:
                    dve.wait_ge(r_in, ph.g(b) * 16 + 16)
                after(dve, xn_done, ph.g(b))
                nc.vector.tensor_tensor(m.y[:].rearrange("p t d -> p (t d)"), m.ps_tail[:],
                                        m.rin[:].rearrange("p t d -> p (t d)"), ALU.add).then_inc(y_done, 1)
                dve.wait_ge(y_done, ph.g(b) + 1)
                dve.sem_inc(tail_free, 1)

            def stats(ph, b):
                tail.start(ph.g(b) * 2)
                nc.vector.bn_stats(m.stats[:, 0, :], m.y[:, 0, :])
                tail.link(nc.vector.bn_stats(m.stats[:, 1, :], m.y[:, 1, :]))
                dve.sem_inc(stats_seen, 1)
                nc.vector.bn_aggr(m.mv[:, 0, :], m.stats[:, 0, :])
                tail.link(nc.vector.bn_aggr(m.mv[:, 1, :], m.stats[:, 1, :]))
                dve.sem_inc(var_done, 1)

            def scale_rows(ph, b):
                dve.wait_ge(rstd_done, ph.g(b) + 1)
                after(dve, xo_done, ph.g(b))
                for t in range(T):
                    last = nc.vector.tensor_scalar(m.xn[:, t, :], m.y[:, t, :], m.mv[:, t, 0:1],
                                                   m.rstd[:, t:t + 1], ALU.subtract, ALU.mult)
                last.then_inc(xn_done, 1)

            nc.vector.memset(m.neg_half[:], -0.5)
            for eps, tile in m.eps.items():
                nc.vector.memset(tile[:], eps)
            nc.vector.memset(m.mparts[:], 0.0)
            for par in range(2):
                last = nc.vector.memset(m.vaug[par][:, :, :, DH:], 1.0)
            last.then_inc(consts_ready, 1)
            dve.wait_ge(consts_ready, 1)
            dve.wait_ge(mask_in, 16)
            nc.vector.tensor_copy(m.maskf[:], m.mask_u8[:]).then_inc(mask_ready, 1)
            dve.wait_ge(mask_ready, 1)
            dve.wait_ge(first_in, 16 * len(first_needed))
            lower_parts(L0, 0, "q")
            dve.wait_ge(now_in, 16 * len(now))
            lower_parts(L0, 0, "k")
            evac_v(L0, 0, 0)
            lower_parts(L0, 1, "q")
            row_max(0, 0)
            row_max(0, 1)
            lower_parts(L0, 1, "k")
            evac_v(L0, 1, 1)
            for u in range(2, NM):
                row_max(0, u)
            split_max(0)

            def step_l0(ph, b, par, first, last):
                front, old = front_target(ph, b, last), tail_target(ph, b, first)

                def maxima(start, end):
                    for u in range(start, end) if not last else ():
                        row_max(b + 1, u)

                if not (first or last):
                    dve.wait_ge(acc_full, ph.g(b) * QUADS)
                    evac_v(ph, b + 1, 1 - par)
                if old:
                    normalise(*old, 0)
                    normalise(*old, 1)
                if front:
                    low_T(*front, "x")
                    lower_parts(*front, "q")
                if last:
                    lower_parts(*front, "k")
                maxima(0, NM)
                if not last:
                    split_max(b + 1)
                if old:
                    add_residual(*old)
                    stats(*old)
                if front and not last:
                    lower_parts(*front, "k")
                if old:
                    scale_rows(*old)

            def step_l1(ph, b, par, first, last):
                front, old = front_target(ph, b, last), tail_target(ph, b, first)
                if front:
                    low_T(*front, "x")
                clip(ph, b, 0)
                clip(ph, b, 1)
                normalise(*old, 0)
                if front and not front[0].own_kv:
                    low_T(*front, "c")
                if front:
                    lower_parts(*front, "q")
                normalise(*old, 1)
                clip(ph, b, 2)
                clip(ph, b, 3)
                if front:
                    lower_parts(*front, "k")
                clip(ph, b, 4)
                clip(ph, b, 5)
                add_residual(*old)
                stats(*old)
                clip(ph, b, 6)
                clip(ph, b, 7)
                scale_rows(*old)

            for ph in phases:
                over_batch(dve, lambda *at: (step_l0 if ph.l0 else step_l1)(ph, *at))
            normalise(ph, B - 1, 0)
            ffn.low_x(dve, 0)
            normalise(ph, B - 1, 1)
            ffn.split_h(dve, 0, 0, True)
            ffn.split_h(dve, 0, 1, True)
            add_residual(ph, B - 1)
            stats(ph, B - 1)
            ffn.split_h(dve, 0, 2, True)
            scale_rows(ph, B - 1)
            for f in range(3, ffn.FT):
                ffn.split_h(dve, 0, f, True)
            ffn.rows(dve, stats_seen)

        @block.gpsimd
        def _(pool):
            tail = Chain(pool, pool_tail)

            def low_part(ph, b, job):
                parts, i = (m.qs, 0) if job == "q" else (m.ks, 1)
                pool.wait_ge(part_m, ph.g(b) * 2 + i + 1)
                nc.gpsimd.tensor_tensor(parts[:, 2], m.rest[i][:], parts[:, 1], ALU.subtract).then_inc(part_l, 1)

            def rstd(ph, b):
                tail.start(ph.g(b) * 2)
                pool.wait_ge(var_done, ph.g(b) + 1)
                tail.link(nc.gpsimd.tensor_tensor(m.vare[:], m.mv[:, :, 1], m.eps[ph.eps][:, 0:T], ALU.add))
                nc.gpsimd.tensor_tensor(m.rstd[:], m.vare[:], m.neg_half[:, 0:T], ALU.pow).then_inc(rstd_done, 1)

            def affine(ph, b):
                tail.start(ph.g(b) * 2 + 1)
                pool.wait_ge(xn_done, ph.g(b) + 1)
                tail.link(nc.gpsimd.tensor_tensor(m.xg[:], m.xn[:], ph.w["gamma"][:], ALU.mult))
                after(pool, x_stored, ph.g(b) * 16)
                nc.gpsimd.tensor_tensor(m.xo[:], m.xg[:], ph.w["beta"][:], ALU.add).then_inc(xo_done, 1)

            def split_weights(ph):
                ph.all_loaded(pool)
                for j, (raw, split) in enumerate(ph.staged):
                    nc.gpsimd.tensor_copy(split[:, 0], raw).then_inc(ph.w_high, 1)
                    pool.wait_ge(ph.w_high, j + 1)
                    nc.gpsimd.tensor_tensor(split[:, 1], raw, split[:, 0].bitcast(F32),
                                            ALU.subtract).then_inc(ph.w_low, 1)

            def residual(ph, b):
                pool.wait_ge(r_in, ph.g(b) * 16 + 16)
                nc.gpsimd.tensor_tensor(m.rin[:], m.rin[:], ph.w["bo"][:], ALU.add).then_inc(resid_ready, 1)

            nc.gpsimd.memset(m.ident_f[:], 0.0)
            nc.gpsimd.memset(m.ident_b[:], 0.0).then_inc(ident_filled, 1)
            pool.wait_ge(ident_filled, 1)
            for ident in (m.ident_f, m.ident_b):
                last = nc.gpsimd.affine_select(out=ident[:], in_=ident[:], compare_op=ALU.not_equal, fill=1.0,
                                               base=0, pattern=[[-1, P]], channel_multiplier=1)
            last.then_inc(ident_ready, 1)
            pool.wait_ge(ident_ready, 1)
            for par in range(2):
                last = nc.gpsimd.memset(m.kp[par][MAX_ROW:MAX_ROW + NPART], 1.0)
            last.then_inc(ones_ready, 1)
            pool.wait_ge(ones_ready, 1)
            pool.wait_ge(consts_ready, 1)
            for b in range(2):
                low_part(L0, b, "q")
                low_part(L0, b, "k")
            def step(ph, b, par, first, last):
                front, old = front_target(ph, b, last), tail_target(ph, b, first)
                if front:
                    low_part(*front, "q")
                if front and (last or not ph.l0):
                    low_part(*front, "k")
                if ph is self_attn and isinstance(b, int):
                    ffn.low_weights(pool, ffn.QUARTER_AT.index(b))
                if old:
                    rstd(*old)
                if front and ph.l0 and not last:
                    low_part(*front, "k")
                if old:
                    affine(*old)
                if ph.l0:
                    residual(ph, b)
                if ph.l0 and isinstance(b, int) and b < 2:
                    split_weights(phases[1 + b])

            for ph in phases:
                ph.all_loaded(pool)
                over_batch(pool, lambda *at: step(ph, *at))
            ffn.weights_split(pool)
            ffn.residual(pool, 0)
            rstd(ph, B - 1)
            affine(ph, B - 1)
            ffn.norm(pool)


class Ffn:

    LAG = 2
    RING = LAG + 1
    PAIR = 2
    NT = PAIR * T
    FT = FF // P
    NSTEP = B // PAIR

    def __init__(self, nc, m, x_src, out, w):
        self.nc, self.m, self.x_src, self.out, self.w = nc, m, x_src, out, w
        self.name, self.loads, self.loaded = "ffn", [], None

    def all_loaded(self, engine):
        engine.wait_ge(self.loaded, 16 * len(self.loads))

    def semaphores(self, sem):
        self.x_in = sem("ffn_x_in")
        self.w_high, self.w_low = sem("ffn_w_high"), sem("ffn_w_low")
        self.xT_full = sem("ffn_xT_full")
        self.x_high, self.x_low = sem("ffn_x_high"), sem("ffn_x_low")
        self.up_full = sem("ffn_up_full")
        self.gelu_done = sem("ffn_gelu_done")
        self.h_high, self.h_low = sem("ffn_h_high"), sem("ffn_h_low")
        self.down_done = sem("ffn_down_done")
        self.y_done = sem("ffn_y_done")
        self.resid_ready = sem("ffn_resid_ready")
        self.stats_done = sem("ffn_stats_done")
        self.var_done = sem("ffn_var_done")
        self.vare_done = sem("ffn_vare_done")
        self.rstd_done = sem("ffn_rstd_done")
        self.xn_done = sem("ffn_xn_done")
        self.xg_done = sem("ffn_xg_done")
        self.xo_done = sem("ffn_xo_done")
        self.stored = sem("ffn_stored")

    def steps(self, engine, step):
        step(0, True, False)
        with engine.Fori(1, self.NSTEP - 1) as i:
            step(i, False, False)
        step(self.NSTEP - 1, False, True)

    def tok(self, dram, i):
        return dram[bass.ds(i * self.PAIR, self.PAIR)].rearrange("a (t p) d -> p (a t) d", p=P)

    QUARTER_AT = (0, 1, B - 2, B - 1)

    def quarter(self, c):
        w = self.m.f_w[c // 2]
        raw = self.m.f_staged[c][:].rearrange("p a n -> p (a n)")
        if c < 2:
            return raw, w[:, 0, c % 2], w[:, 1, c % 2]
        return raw, w[:, 0, c % 2].rearrange("p a n -> p (a n)"), w[:, 1, c % 2].rearrange("p a n -> p (a n)")

    def high_weights(self, act, c):
        raw, high, _ = self.quarter(c)
        self.all_loaded(act)
        self.nc.scalar.copy(high, raw).then_inc(self.w_high, 1)

    def low_weights(self, pool, c):
        raw, high, low = self.quarter(c)
        pool.wait_ge(self.w_high, c + 1)
        self.nc.gpsimd.tensor_tensor(low, raw, high.bitcast(F32), ALU.subtract).then_inc(self.w_low, 1)

    def weights_split(self, engine):
        engine.wait_ge(self.w_low, 4)

    def load(self, sp, seen, i, x_stored, before):
        if isinstance(i, int) and i == 0:
            reached(sp, seen, self.w_low, 4)
        reached(sp, seen, x_stored, (before + i * self.PAIR + self.PAIR) * 16)
        sp.dma_start(self.m.f_x[:], self.tok(self.x_src, i)).then_inc(self.x_in, 16)

    def load_and_store(self, sp, seen, x_stored, before):
        def store(i):
            reached(sp, seen, self.xo_done, i + 1)
            sp.dma_start(self.tok(self.out, i), self.m.f_xo[:]).then_inc(self.stored, 16)

        def step(i, first, last):
            if not last:
                reached(sp, seen, self.xT_full, i * self.PAIR + self.PAIR)
                reached(sp, seen, self.resid_ready, i + 1)
                self.load(sp, seen, i + 1, x_stored, before)
            if not first:
                store(i - 1)

        self.steps(sp, step)
        for a in range(self.PAIR):
            i = self.NSTEP - 1
            reached(sp, seen, self.xo_done, i + a + 1)
            sp.dma_start(self.tok(self.out, i)[:, a * T:(a + 1) * T],
                         self.m.f_xo[:, a * T:(a + 1) * T]).then_inc(self.stored, 16)
        reached(sp, seen, self.stored, 16 * (self.NSTEP - 1 + self.PAIR))

    def transposes(self, pe, i):
        nc, m = self.nc, self.m
        pe.wait_ge(self.x_in, i * 16 + 16)
        for a in range(self.PAIR):
            for t in range(T):
                for k in range(KT):
                    last = nc.tensor.transpose(m.ps_scores[:, a, k * S + t * P:k * S + (t + 1) * P],
                                               m.f_x[:, a * T + t, k * P:(k + 1) * P], m.ident_f[:])
            last.then_inc(self.xT_full, 1)

    def up(self, pe, i, f, first):
        m = self.m
        if f == 0:
            pe.wait_ge(self.x_low, i * self.PAIR + self.PAIR)
        if not (first and f < 2):
            pe.wait_ge(self.gelu_done, i * self.FT + f - 1)
        products = [(k, wp, xp) for k in range(KT) for wp, xp in PASSES]
        for n, (k, wp, xp) in enumerate(products):
            mm = self.nc.tensor.matmul(m.ps_scores[:, 2 + f % 2, :], m.f_w1[:, wp, k, f * P:(f + 1) * P],
                                       m.f_xT[:, xp, k, :], start=(n == 0), stop=(n == len(products) - 1))
        mm.then_inc(self.up_full, 1)

    def down(self, pe, i, f, first):
        m = self.m
        pe.wait_ge(self.h_low, i * self.FT + f + 1)
        if f == 0 and not first:
            pe.wait_ge(self.y_done, i * self.PAIR)
        for t in range(self.NT):
            for n, (hp, wp) in enumerate(PASSES):
                first_of_bank, last_of_bank = (t % T, n) == (0, 0), (t % T, n) == (T - 1, len(PASSES) - 1)
                mm = self.nc.tensor.matmul(m.ps_down[t // T][:, (t % T) * D:(t % T + 1) * D],
                                           m.f_h[:, hp, f % self.RING, t * P:(t + 1) * P], m.f_w2[:, wp, f // 4, f % 4, :],
                                           start=(f == 0 and first_of_bank), stop=(f == self.FT - 1 and last_of_bank))
        mm.then_inc(self.down_done, 1)

    def products(self, pe):
        def step(i, first, last):
            if not first:
                for f in range(self.FT):
                    if f == self.FT - 1 and not last:
                        self.transposes(pe, i + 1)
                    self.up(pe, i, f, False)
                    if f >= self.LAG:
                        self.down(pe, i, f - self.LAG, False)
            for f in range(self.FT - self.LAG, self.FT):
                self.down(pe, i, f, first)

        self.steps(pe, step)

    def evac_x(self, act, i):
        nc, m = self.nc, self.m
        for a in range(self.PAIR):
            act.wait_ge(self.xT_full, i * self.PAIR + a + 1)
            if a == 0 and not (isinstance(i, int) and i == 0):
                act.wait_ge(self.up_full, i * self.FT)
            nc.scalar.copy(m.f_xT[:, 0, :, a * S:(a + 1) * S],
                           m.ps_scores[:, a, :].rearrange("p (k n) -> p k n", k=KT)).then_inc(self.x_high, 1)

    def gelu(self, act, i, f, first):
        m = self.m
        act.wait_ge(self.up_full, i * self.FT + f + 1)
        if not (first and f < 2):
            act.wait_ge(self.h_low, i * self.FT + f - 1)
        self.nc.scalar.activation(m.f_g[:, f % 2, :], m.ps_scores[:, 2 + f % 2, :], ACT.Gelu,
                                  bias=self.w["b1"][:, f:f + 1]).then_inc(self.gelu_done, 1)

    def gelus(self, act):
        def step(i, first, last):
            if not first:
                for f in range(self.FT):
                    self.gelu(act, i, f, False)
            if not last:
                self.evac_x(act, i + 1)

        self.steps(act, step)

    def low_x(self, dve, i):
        nc, m = self.nc, self.m
        for a in range(self.PAIR):
            dve.wait_ge(self.x_high, i * self.PAIR + a + 1)
            at = slice(a * S, (a + 1) * S)
            nc.vector.tensor_tensor(m.f_xT[:, 1, :, at], m.ps_scores[:, a, :].rearrange("p (k n) -> p k n", k=KT),
                                    m.f_xT[:, 0, :, at].bitcast(F32), ALU.subtract).then_inc(self.x_low, 1)

    def split_h(self, dve, i, f, first):
        nc, m = self.nc, self.m
        dve.wait_ge(self.gelu_done, i * self.FT + f + 1)
        if f >= self.RING or not first:
            dve.wait_ge(self.down_done, i * self.FT + max(f - self.LAG, 0))
        high, low = m.f_h[:, 0, f % self.RING, :], m.f_h[:, 1, f % self.RING, :]
        nc.vector.tensor_copy(high, m.f_g[:, f % 2, :]).then_inc(self.h_high, 1)
        dve.wait_ge(self.h_high, i * self.FT + f + 1)
        nc.vector.tensor_tensor(low, m.f_g[:, f % 2, :], high.bitcast(F32), ALU.subtract).then_inc(self.h_low, 1)

    def add_residual(self, dve, i, first):
        nc, m = self.nc, self.m
        dve.wait_ge(self.down_done, i * self.FT + self.FT)
        dve.wait_ge(self.resid_ready, i + 1)
        if not first:
            dve.wait_ge(self.xo_done, i)
        for a in range(self.PAIR):
            nc.vector.tensor_tensor(m.f_y[:, a * T:(a + 1) * T].rearrange("p t d -> p (t d)"), m.ps_down[a],
                                    m.f_r[:, a * T:(a + 1) * T].rearrange("p t d -> p (t d)"),
                                    ALU.add).then_inc(self.y_done, 1)

    def stats(self, dve, seen, i):
        nc, m = self.nc, self.m
        dve.wait_ge(self.y_done, i * self.PAIR + self.PAIR)
        for t in range(self.NT):
            last = nc.vector.bn_stats(m.f_stats[:, t, :], m.f_y[:, t, :])
        last.then_inc(self.stats_done, 1)
        dve.wait_ge(self.stats_done, i + 1)
        dve.sem_inc(seen, 1)
        for t in range(self.NT):
            last = nc.vector.bn_aggr(m.f_mv[:, t, :], m.f_stats[:, t, :])
        last.then_inc(self.var_done, 1)

    def scale_rows(self, dve, i):
        nc, m = self.nc, self.m
        dve.wait_ge(self.rstd_done, i + 1)
        for t in range(self.NT):
            xn = nc.vector.tensor_scalar(m.f_y[:, t, :], m.f_y[:, t, :], m.f_mv[:, t, 0:1],
                                         m.f_rstd[:, t:t + 1], ALU.subtract, ALU.mult)
        xn.then_inc(self.xn_done, 1)

    def rows(self, dve, seen):
        def step(i, first, last):
            for f in range(self.FT) if not first else ():
                self.split_h(dve, i, f, False)
                if f == 1:
                    self.stats(dve, seen, i - 1)
                if f == 4:
                    self.scale_rows(dve, i - 1)
            if not last:
                self.low_x(dve, i + 1)
            self.add_residual(dve, i, first)

        self.steps(dve, step)
        self.stats(dve, seen, self.NSTEP - 1)
        self.scale_rows(dve, self.NSTEP - 1)
        nc, m, w = self.nc, self.m, self.w
        dve.wait_ge(self.xn_done, self.NSTEP)
        dve.wait_ge(self.stored, 16 * (self.NSTEP - 1))
        for a in range(self.PAIR):
            at = slice(a * T, (a + 1) * T)
            nc.vector.tensor_tensor(m.f_y[:, at], m.f_y[:, at], w["gamma"][:], ALU.mult).then_inc(self.xg_done, 1)
            dve.wait_ge(self.xg_done, self.NSTEP + a)
            nc.vector.tensor_tensor(m.f_xo[:, at], m.f_y[:, at], w["beta"][:], ALU.add).then_inc(self.xo_done, 1)

    def residual(self, pool, i):
        nc, m = self.nc, self.m
        pool.wait_ge(self.x_in, i * 16 + 16)
        for a in range(self.PAIR):
            r = nc.gpsimd.tensor_tensor(m.f_r[:, a * T:(a + 1) * T], m.f_x[:, a * T:(a + 1) * T],
                                        self.w["b2"][:], ALU.add)
        r.then_inc(self.resid_ready, 1)

    def norm(self, pool):
        nc, m, w = self.nc, self.m, self.w

        def step(i, first, last):
            if not last:
                pool.wait_ge(self.y_done, i * self.PAIR + self.PAIR)
                self.residual(pool, i + 1)
            pool.wait_ge(self.var_done, i + 1)
            nc.gpsimd.tensor_tensor(m.f_vare[:], m.f_mv[:, :, 1], m.eps[1e-5][:], ALU.add).then_inc(self.vare_done, 1)
            pool.wait_ge(self.vare_done, i + 1)
            nc.gpsimd.tensor_tensor(m.f_rstd[:], m.f_vare[:], m.neg_half[:], ALU.pow).then_inc(self.rstd_done, 1)
            if last:
                return
            pool.wait_ge(self.xn_done, i + 1)
            for a in range(self.PAIR):
                y = m.f_y[:, a * T:(a + 1) * T]
                g = nc.gpsimd.tensor_tensor(y, y, w["gamma"][:], ALU.mult)
            g.then_inc(self.xg_done, 1)
            pool.wait_ge(self.xg_done, i + 1)
            if not first:
                pool.wait_ge(self.stored, i * 16)
            for a in range(self.PAIR):
                o = nc.gpsimd.tensor_tensor(m.f_xo[:, a * T:(a + 1) * T], m.f_y[:, a * T:(a + 1) * T],
                                            w["beta"][:], ALU.add)
            o.then_inc(self.xo_done, 1)

        self.steps(pool, step)


class Memory:
    pass


def build(nc, a, out):
    with ExitStack() as ctx:
        def sb(name, shape, dt=F32):
            return ctx.enter_context(nc.sbuf_tensor(name, shape, dt))

        def pair(name, shape, dt):
            return [sb(f"{name}{i}", shape, dt) for i in range(2)]

        m = Memory()
        m.ident_f, m.ident_b = sb("ident_f", [P, P]), sb("ident_b", [P, P], BF16)
        m.mask_u8, m.maskf = sb("mask_u8", [P, B, T], U8), sb("maskf", [P, B, T])
        m.neg_half = sb("neg_half", [P, 2 * T])
        m.eps = {1e-6: sb("eps_l0", [P, 2 * T]), 1e-5: sb("eps_l1", [P, 2 * T])}
        m.xin, m.cin, m.rin = sb("xin", [P, T, D]), sb("cin", [P, T, D]), sb("rin", [P, T, D])
        m.qs, m.ks = sb("q_parts", [P, NPART, KT, S], BF16), sb("k_parts", [P, NPART, KT, S], BF16)
        m.rest = pair("rest", [P, KT, S], F32)
        m.vaug = pair("v_ones", [P, T, H, 32], F32)
        m.probs = pair("probs", [P, 4, T, S], F32)
        m.acc = sb("acc", [P, QUADS, S])
        m.rmax, m.rrest = sb("rmax", [P, T, H]), sb("rmax_rest", [P, T, H])
        m.mparts, m.maxT = sb("max_parts", [P, T, P // H, H], BF16), sb("maxT", [NPART * H, S], BF16)
        m.den, m.den2, m.rden, m.rden2 = (sb(n, [P, T, H // 2]) for n in ("den", "den2", "rden", "rden2"))
        m.ctx = sb("ctx", [P, T, D])
        m.y, m.xn, m.xg, m.xo = (sb(n, [P, T, D]) for n in ("y", "xn", "xg", "xo"))
        m.stats, m.mv = sb("stats", [P, T, 6]), sb("mv", [P, T, 2])
        m.vare, m.rstd = sb("vare", [P, T]), sb("rstd", [P, T])
        m.f_x, m.f_r, m.f_y, m.f_xo = (sb(f"f_{n}", [P, 2 * T, D]) for n in ("x", "r", "y", "xo"))
        m.f_staged = m.f_x, m.f_r, m.f_y, m.f_xo
        m.f_w1 = sb("f_w1", [P, 2, KT, FF], F32R)
        m.f_w2 = sb("f_w2", [P, 2, 2, FF // P // 2, D], F32R)
        m.f_w = m.f_w1, m.f_w2
        m.f_stats, m.f_mv = sb("f_stats", [P, 2 * T, 6]), sb("f_mv", [P, 2 * T, 2])
        m.f_vare, m.f_rstd = sb("f_vare", [P, 2 * T]), sb("f_rstd", [P, 2 * T])
        m.ps_scores = ctx.enter_context(nc.psum_tensor("ps_scores", [P, 4, 512], F32))
        m.ps_acc = ctx.enter_context(nc.psum_tensor("ps_acc", [P, 512], F32))
        m.ps_front = ctx.enter_context(nc.psum_tensor("ps_front", [P, 2, 512], F32))
        m.ps_down = m.ps_acc[:], m.ps_front[:, 0]
        m.ps_tail = ctx.enter_context(nc.psum_tensor("ps_tail", [P, 512], F32))
        x1 = nc.dram_tensor("x_after_l0", (B, S, D), F32, kind="Internal").ap()
        x2 = nc.dram_tensor("x_after_self", (B, S, D), F32, kind="Internal").ap()
        x3 = nc.dram_tensor("x_after_cross", (B, S, D), F32, kind="Internal").ap()

        def mat(name, dram):
            n = dram.shape[1]
            t = sb(name, [P, dram.shape[0] // P, n])
            return t, (t[:], dram.rearrange("(k p) n -> p k n", p=P))

        def cols(name, vec):
            t = sb(name, [P, vec.shape[0] // P])
            return t, (t[:], vec.rearrange("(m p) -> p m", p=P))

        def row(name, vec):
            t = sb(name, [P, 1, D])
            src = vec.rearrange("(o t d) -> o t d", o=1, t=1).to_broadcast((P, 1, D))
            return t[:].to_broadcast((P, T, D)), (t[:], src)

        def weights(prefix, names, kind_cols=(), kind_rows=()):
            w, loads = {}, []
            for key, name in names:
                w[key], load = mat(f"{prefix}_{key}", a[name])
                loads.append(load)
            for key, name in kind_cols:
                w[key], load = cols(f"{prefix}_{key}", a[name])
                loads.append(load)
            for key, name in kind_rows:
                w[key], load = row(f"{prefix}_{key}", a[name])
                loads.append(load)
            return w, loads

        w0, l0q = weights("l0", [("q", "L0_xattn_Wq")], [("bq", "L0_xattn_bq")])
        w0k, l0 = weights("l0", [("k", "L0_xattn_Wk"), ("v", "L0_xattn_Wv")], [("bk", "L0_xattn_bk")],
                          [("bv", "L0_xattn_bv")])
        w0o, l0o = weights("l0", [("o", "L0_xattn_Wo")], (),
                           [("bo", "L0_xattn_bo"), ("gamma", "L0_xattn_gamma"), ("beta", "L0_xattn_beta")])
        w0.update(w0k)
        w0.update(w0o)
        ws, ls = weights("sa", [("o", "L1_xattn_sa_wo")], (),
                         [("gamma", "L1_xattn_g1"), ("beta", "L1_xattn_be1")])
        wc, lc = weights("ca", [("q", "L1_xattn_ca_wq"), ("o", "L1_xattn_ca_wo")], (),
                         [("gamma", "L1_xattn_g2"), ("beta", "L1_xattn_be2")])
        wf, lf = weights("ff", (), [("b1", "L1_xattn_b1")],
                         [("b2", "L1_xattn_b2"), ("gamma", "L1_xattn_g3"), ("beta", "L1_xattn_be3")])
        w1, w2 = a["L1_xattn_w1"], a["L1_xattn_w2"]
        for c in range(4):
            half = bass.ds((c % 2) * 4 * P, 4 * P)
            src = w1[(c % 2) * P:(c % 2 + 1) * P].rearrange("p (a n) -> p a n", n=D) if c < 2 else (
                w2[half].rearrange("(a p) n -> p a n", p=P))
            lf.append((m.f_staged[c][:], src))
        m.mask_load = m.mask_u8[:], a["mask_BxS_bf1"].rearrange("b (t p) -> p b t", p=P)

        ctx.enter_context(nc.allow_non_contiguous_dma(reason="biases and the mask are laid out once"))
        ctx_in = a["ctx_1024"]
        cross0 = Attention(None, "l0", a["x"], ctx_in, x1, w0, l0=True, eps=1e-6)
        self_attn = Attention(cross0, "sa", x1, None, x2, ws, masked=True)
        cross1 = Attention(self_attn, "ca", x2, ctx_in, x3, wc)
        xT, cT, split_T = sb("xT", [P, KT, S]), sb("cT", [P, KT, S]), sb("split_T", [P, 2, KT, S], F32R)
        m.ctxT = sb("ctxT", [P, KT, S])
        cross0.xT, cross0.cT = xT, cT
        self_attn.xT, self_attn.cT = split_T, None
        cross1.xT, cross1.cT = xT, split_T
        for ph, loads, stage in ((self_attn, ls, m.f_staged[:2]), (cross1, lc, m.f_staged[2:])):
            for j, key in enumerate(ph.split_keys):
                raw = stage[j // 2][:, (j % 2) * KT:(j % 2 + 1) * KT]
                ph.w[key] = sb(f"{ph.name}_{key}", [P, 2, KT, D], F32R)
                loads.append((raw, a[f"L1_xattn_{ph.name}_w{key}"].rearrange("(k p) n -> p k n", p=P)))
                ph.staged.append((raw, ph.w[key]))
        with ExitStack() as packed:
            m.qp, m.kp = ([packed.enter_context(nc.sbuf_tensor(f"{n}_packed{i}", [P, H, S], BF16))
                           for i in range(2)] for n in "qk")
        ffn_ring = Ffn.RING
        m.f_xT = sb("f_xT", [P, 2, KT, 2 * S], F32R)
        m.f_h = sb("f_h", [P, 2, ffn_ring, 2 * S], F32R)
        m.f_g = sb("f_g", [P, 2, 2 * S])
        ffn = Ffn(nc, m, x3, out, wf)
        for group, loads in ((cross0, l0o), (self_attn, ls), (cross1, lc), (ffn, lf)):
            group.loads = loads
        attention(nc, m, [cross0, self_attn, cross1], l0q, l0, ffn)


_INS = ["x", "ctx_1024", "mask_BxS_bf1",
        "L0_xattn_Wv", "L0_xattn_bv", "L0_xattn_Wk", "L0_xattn_bk", "L0_xattn_Wq", "L0_xattn_bq",
        "L0_xattn_Wo", "L0_xattn_bo", "L0_xattn_gamma", "L0_xattn_beta",
        "L1_xattn_sa_wq", "L1_xattn_sa_wk", "L1_xattn_sa_wv", "L1_xattn_sa_wo",
        "L1_xattn_ca_wq", "L1_xattn_ca_wk", "L1_xattn_ca_wv", "L1_xattn_ca_wo",
        "L1_xattn_w1", "L1_xattn_b1", "L1_xattn_w2", "L1_xattn_b2",
        "L1_xattn_g1", "L1_xattn_be1", "L1_xattn_g2", "L1_xattn_be2", "L1_xattn_g3", "L1_xattn_be3"]


_BY_HEAD_PAIR = ("L0_xattn_Wq", "L0_xattn_bq", "L0_xattn_Wk", "L0_xattn_bk",
                 "L1_xattn_sa_wq", "L1_xattn_sa_wk", "L1_xattn_ca_wq", "L1_xattn_ca_wk")


def kernel(**inputs):
    import numpy as _np
    import concourse.bacc as _bacc
    from concourse import mybir as _mybir
    from concourse.bass_utils import run_bass_kernel_spmd as _run

    nc = _bacc.Bacc("TRN2", target_bir_lowering=False, num_devices=1)
    arrays, args = {}, {}
    for name in _INS:
        v = inputs[name]
        if name in _BY_HEAD_PAIR:
            lead = v.shape[:-1]
            v = _np.moveaxis(_np.reshape(v, lead + (H // 2, 2, DH)), -3, -1).reshape(lead + (D,))
        v = _np.ascontiguousarray(v)
        if v.dtype == _np.bool_:
            v = v.view(_np.uint8)
        arrays[f"in_{name}"] = v
        args[name] = nc.dram_tensor(f"in_{name}", v.shape, _mybir.dt.from_np(v.dtype), kind="ExternalInput").ap()
    out = nc.dram_tensor("out_0", (B, S, D), F32, kind="ExternalOutput").ap()
    build(nc, args, out)
    r = _run(nc, [arrays], core_ids=[0])
    return r.results[0]["out_0"]
```
